# Optimizing a Trainium2 kernel written in Bass

```python
import numpy as np
import jax
import jax.numpy as jnp

def _softmax(x, axis=-1):
    return jax.nn.softmax(x, axis=axis)

def _gelu(x):
    return jax.nn.gelu(x, approximate=True)

def _silu(x):
    return jax.nn.silu(x)

def _sigmoid(x):
    return jax.nn.sigmoid(x)

def _layernorm(x, axis=-1, eps=1e-05):
    m = jnp.mean(x, axis=axis, keepdims=True)
    v = jnp.var(x, axis=axis, keepdims=True)
    return (x - m) / jnp.sqrt(v + eps)

def _scatter_add(tgt, idx, src, axis=0):
    return tgt.at[idx].add(src)

def _segment_sum(src, seg, n):
    return jax.ops.segment_sum(src, seg, n)
kernel_name = 'mk_gnn_resnorm_d4_gnn_r64_a2adcb'

def setup_inputs(seed: int=0):
    np.random.seed(seed)
    _w = jnp.asarray

    def _rec_inputs():
        import jax
        import jax.numpy as jnp
        _gk = jax.random.key(seed)
        x = -0.000202 + 1 * jax.random.normal(jax.random.fold_in(_gk, 1), (50000, 160), jnp.float32)
        src = jax.random.randint(jax.random.fold_in(_gk, 2), (25000,), 0, 50000, jnp.int32)
        dst = jnp.minimum((50000 * jax.random.uniform(jax.random.fold_in(_gk, 3), (25000,)) ** 2.0).astype(jnp.int32), 49999)
        _o = jnp.argsort(dst, stable=True)
        src = src[_o]
        dst = dst[_o]
        edge_attr_10 = jax.random.uniform(jax.random.fold_in(_gk, 12), (25000, 10), jnp.float32, 0.0, 1)
        edge_attr_16 = -0.000191324 + 0.999809 * jax.random.normal(jax.random.fold_in(_gk, 13), (25000, 16), jnp.float32)
        edge_attr_4 = -0.000414295 + 0.999828 * jax.random.normal(jax.random.fold_in(_gk, 14), (25000, 4), jnp.float32)
        edge_attr_8 = jax.random.uniform(jax.random.fold_in(_gk, 15), (25000, 8), jnp.float32, 0.0, 1)
        node_vec1 = jax.random.uniform(jax.random.fold_in(_gk, 16), (50000, 1), jnp.float32, 0.0, 1)
        node_vec1_n2 = jax.random.uniform(jax.random.fold_in(_gk, 17), (50000, 1), jnp.float32, 0.0, 1)
        node_vec1_n3 = jax.random.uniform(jax.random.fold_in(_gk, 18), (50000, 1), jnp.float32, 0.0, 1)
        return (x, src, dst, edge_attr_10, edge_attr_16, edge_attr_4, edge_attr_8, node_vec1, node_vec1_n2, node_vec1_n3)
    x, src, dst, edge_attr_10, edge_attr_16, edge_attr_4, edge_attr_8, node_vec1, node_vec1_n2, node_vec1_n3 = _rec_inputs()

    def _L0_gnn_setup():
        import jax, jax.numpy as jnp
        import numpy as np
        N = 625
        E = 6250
        MUL0, MUL1 = (64, 32)
        RAD, HID = (8, 64)
        WNUM = 192
        NUM_NEIGHBORS = 10.0
        INV3 = 1.0 / np.sqrt(3.0)

        def _lin(s, v, Ws, Wv, attr):
            out_s = s @ Ws * attr * (1.0 / np.sqrt(Ws.shape[0]))
            out_v = jnp.einsum('nud,uv->nvd', v, Wv) * attr[..., None] * (1.0 / np.sqrt(Wv.shape[0]))
            return (out_s, out_v)
        key = jax.random.key(seed)
        ks = jax.random.split(key, 16)
        return {'node_input': jax.random.normal(ks[0], (N, MUL0 + 3 * MUL1), jnp.float32), 'node_attr': jnp.ones((N, 1), jnp.float32), 'edge_attr': jax.random.normal(ks[1], (E, 4), jnp.float32), 'edge_scalars': jax.random.uniform(ks[2], (E, RAD), jnp.float32), 'W_sc_s': jax.random.normal(ks[3], (MUL0, MUL0), jnp.float32), 'W_sc_v': jax.random.normal(ks[4], (MUL1, MUL1), jnp.float32), 'W1_s': jax.random.normal(ks[5], (MUL0, MUL0), jnp.float32), 'W1_v': jax.random.normal(ks[6], (MUL1, MUL1), jnp.float32), 'W2_s': jax.random.normal(ks[7], (MUL0 + MUL1, MUL0), jnp.float32), 'W2_v': jax.random.normal(ks[8], (MUL0 + MUL1, MUL1), jnp.float32), 'W3': jax.random.normal(ks[9], (MUL0 + MUL1, 1), jnp.float32), 'fcW1': jax.random.normal(ks[10], (RAD, HID), jnp.float32), 'fcW2': jax.random.normal(ks[11], (HID, WNUM), jnp.float32), 'edge_src': jax.random.randint(ks[12], (E,), 0, N, jnp.int32), 'edge_dst': jax.random.randint(ks[13], (E,), 0, N, jnp.int32)}
    _L0_gnn_all = _L0_gnn_setup()
    _L0_gnn_in = {k: v for k, v in _L0_gnn_all.items() if k in ('W_sc_s', 'W_sc_v', 'W1_s', 'W1_v', 'W2_s', 'W2_v', 'W3', 'fcW1', 'fcW2')}
    del _L0_gnn_all

    def _L1_gnn_setup():
        import jax, jax.numpy as jnp
        import numpy as np
        N_NODES = 50000
        N_EDGES = 12500
        MUL0, MUL1 = (64, 32)
        N_BASIS, N_RADIAL = (10, 100)
        W_NUMEL = 192
        NUM_NEIGHBORS = 16.0
        INV_SQRT3 = np.float32(1.0 / np.sqrt(3.0))
        RELU_GAIN = np.float32(np.sqrt(2.0))
        FAN_L2 = np.float32(np.sqrt(MUL0 + MUL1))

        def _fctp_scalar_attr(x0, x1, a, W0, W1):
            o0 = x0 @ W0 * a * (1.0 / np.sqrt(W0.shape[0]))
            o1 = jnp.einsum('nud,uw->nwd', x1, W1) * a[..., None] * (1.0 / np.sqrt(W1.shape[0]))
            return (o0, o1)
        key = jax.random.key(seed)
        ks = jax.random.split(key, 16)
        return {'node_input': jax.random.normal(ks[0], (N_NODES, MUL0 + 3 * MUL1), jnp.float32), 'node_attr': jnp.ones((N_NODES, 1), jnp.float32), 'edge_attr': jax.random.normal(ks[1], (N_EDGES, 4), jnp.float32), 'edge_length_embedded': jax.random.uniform(ks[2], (N_EDGES, N_BASIS), dtype=jnp.float32), 'W_si0': jax.random.normal(ks[3], (MUL0, MUL0), jnp.float32), 'W_si1': jax.random.normal(ks[4], (MUL1, MUL1), jnp.float32), 'W_l1_0': jax.random.normal(ks[5], (MUL0, MUL0), jnp.float32), 'W_l1_1': jax.random.normal(ks[6], (MUL1, MUL1), jnp.float32), 'W_l2_00': jax.random.normal(ks[7], (MUL0, MUL0), jnp.float32), 'W_l2_10': jax.random.normal(ks[8], (MUL1, MUL0), jnp.float32), 'W_l2_01': jax.random.normal(ks[9], (MUL0, MUL1), jnp.float32), 'W_l2_11': jax.random.normal(ks[10], (MUL1, MUL1), jnp.float32), 'W_fc1': jax.random.normal(ks[11], (N_BASIS, N_RADIAL), jnp.float32), 'W_fc2': jax.random.normal(ks[12], (N_RADIAL, W_NUMEL), jnp.float32), 'edge_src': jax.random.randint(ks[13], (N_EDGES,), 0, N_NODES), 'edge_dst': jax.random.randint(ks[14], (N_EDGES,), 0, N_NODES)}
    _L1_gnn_all = _L1_gnn_setup()
    _L1_gnn_in = {k: v for k, v in _L1_gnn_all.items() if k in ('W_si0', 'W_si1', 'W_l1_0', 'W_l1_1', 'W_l2_00', 'W_l2_10', 'W_l2_01', 'W_l2_11', 'W_fc1', 'W_fc2')}
    del _L1_gnn_all

    def _L2_gnn_setup():
        import jax, jax.numpy as jnp
        import numpy as np
        N = 20000
        E = 5000
        MUL0 = 64
        MUL1 = 32
        FC_IN = 16
        FC_H = 64
        WNUM = 192
        key = jax.random.key(seed)
        ks = jax.random.split(key, 16)
        return {'x': jax.random.normal(ks[0], (N, MUL0 + 3 * MUL1), jnp.float32), 'node_attr': jnp.ones((N, 1), jnp.float32), 'edge_scalars': jax.random.normal(ks[1], (E, FC_IN), jnp.float32), 'edge_attr_sh': jax.random.normal(ks[2], (E, 4), jnp.float32), 'edge_src': jax.random.randint(ks[3], (E,), 0, N), 'edge_dst': jax.random.randint(ks[4], (E,), 0, N), 'Wfc1': jax.random.normal(ks[5], (FC_IN, FC_H), jnp.float32), 'Wfc2': jax.random.normal(ks[6], (FC_H, WNUM), jnp.float32), 'Wsc0': jax.random.normal(ks[7], (MUL0, MUL0), jnp.float32), 'Wsc1': jax.random.normal(ks[8], (MUL1, MUL1), jnp.float32), 'Wl1_0': jax.random.normal(ks[9], (MUL0, MUL0), jnp.float32), 'Wl1_1': jax.random.normal(ks[10], (MUL1, MUL1), jnp.float32), 'Wl2_s': jax.random.normal(ks[11], (MUL0 + MUL1, MUL0), jnp.float32), 'Wl2_v': jax.random.normal(ks[12], (MUL0 + MUL1, MUL1), jnp.float32), 'Wa': 0.1 * jax.random.normal(ks[13], (MUL0 + MUL1, 1), jnp.float32)}
    _L2_gnn_all = _L2_gnn_setup()
    _L2_gnn_in = {k: v for k, v in _L2_gnn_all.items() if k in ('Wfc1', 'Wfc2', 'Wsc0', 'Wsc1', 'Wl1_0', 'Wl1_1', 'Wl2_s', 'Wl2_v', 'Wa')}
    del _L2_gnn_all

    def _L3_gnn_setup():
        import jax, jax.numpy as jnp
        import numpy as np
        N = 25000
        E = 6250
        S = 64
        V = 32
        NB = 10
        H = 100
        WN = 192
        MID = 96
        NUM_NEIGHBORS = 16.0
        C_S = float(np.sin(np.pi / 8.0))
        C_X = float(np.cos(np.pi / 8.0))
        SQRT3 = float(np.sqrt(3.0))

        def fctp_scalar_attr(xs, xv, attr, Ws, Wv):
            s = xs * attr @ Ws
            v = jnp.einsum('nuc,uo->noc', xv * attr[:, :, None], Wv)
            return (s, v)
        key = jax.random.key(seed)
        k = jax.random.split(key, 24)

        def w(i, shape):
            return jax.random.normal(k[i], shape, jnp.float32) / np.sqrt(float(shape[0]))
        return {'node_input': jax.random.normal(k[0], (N, S + 3 * V), jnp.float32), 'node_attr': jax.random.normal(k[1], (N, 1), jnp.float32), 'node_crystal_attr': jax.random.normal(k[2], (N, 1), jnp.float32), 'sym_mask': jax.random.normal(k[3], (N, 1), jnp.float32), 'edge_attr': jax.random.normal(k[4], (E, 4), jnp.float32), 'edge_length_embedded': jax.random.uniform(k[5], (E, NB), dtype=jnp.float32), 'edge_src': jax.random.randint(k[6], (E,), 0, N), 'edge_dst': jax.random.randint(k[7], (E,), 0, N), 'Ws_sc_a': w(8, (S, S)), 'Wv_sc_a': w(9, (V, V)), 'Ws_sc_c': w(10, (S, S)), 'Wv_sc_c': w(11, (V, V)), 'Ws_l1_a': w(12, (S, S)), 'Wv_l1_a': w(13, (V, V)), 'Ws_l1_c': w(14, (S, S)), 'Wv_l1_c': w(15, (V, V)), 'W_fc1': w(16, (NB, H)), 'W_fc2': w(17, (H, WN)), 'Ws_l2_a': w(18, (MID, MID)), 'Wv_l2_a': w(19, (MID, MID)), 'Ws_l2_c': w(20, (MID, MID)), 'Wv_l2_c': w(21, (MID, MID)), 'Ws_l3': w(22, (MID, S)), 'Wv_l3': w(23, (MID, V))}
    _L3_gnn_all = _L3_gnn_setup()
    _L3_gnn_in = {k: v for k, v in _L3_gnn_all.items() if k in ('Ws_sc_a', 'Wv_sc_a', 'Ws_sc_c', 'Wv_sc_c', 'Ws_l1_a', 'Wv_l1_a', 'Ws_l1_c', 'Wv_l1_c', 'W_fc1', 'W_fc2', 'Ws_l2_a', 'Wv_l2_a', 'Ws_l2_c', 'Wv_l2_c', 'Ws_l3', 'Wv_l3')}
    del _L3_gnn_all
    return {'x': x, 'src': src, 'dst': dst, 'edge_attr_10': edge_attr_10, 'edge_attr_16': edge_attr_16, 'edge_attr_4': edge_attr_4, 'edge_attr_8': edge_attr_8, 'node_vec1': node_vec1, 'node_vec1_n2': node_vec1_n2, 'node_vec1_n3': node_vec1_n3, 'L0_gnn_W_sc_s': _L0_gnn_in['W_sc_s'], 'L0_gnn_W_sc_v': _L0_gnn_in['W_sc_v'], 'L0_gnn_W1_s': _L0_gnn_in['W1_s'], 'L0_gnn_W1_v': _L0_gnn_in['W1_v'], 'L0_gnn_W2_s': _L0_gnn_in['W2_s'], 'L0_gnn_W2_v': _L0_gnn_in['W2_v'], 'L0_gnn_W3': _L0_gnn_in['W3'], 'L0_gnn_fcW1': _L0_gnn_in['fcW1'], 'L0_gnn_fcW2': _L0_gnn_in['fcW2'], 'L1_gnn_W_si0': _L1_gnn_in['W_si0'], 'L1_gnn_W_si1': _L1_gnn_in['W_si1'], 'L1_gnn_W_l1_0': _L1_gnn_in['W_l1_0'], 'L1_gnn_W_l1_1': _L1_gnn_in['W_l1_1'], 'L1_gnn_W_l2_00': _L1_gnn_in['W_l2_00'], 'L1_gnn_W_l2_10': _L1_gnn_in['W_l2_10'], 'L1_gnn_W_l2_01': _L1_gnn_in['W_l2_01'], 'L1_gnn_W_l2_11': _L1_gnn_in['W_l2_11'], 'L1_gnn_W_fc1': _L1_gnn_in['W_fc1'], 'L1_gnn_W_fc2': _L1_gnn_in['W_fc2'], 'L2_gnn_Wfc1': _L2_gnn_in['Wfc1'], 'L2_gnn_Wfc2': _L2_gnn_in['Wfc2'], 'L2_gnn_Wsc0': _L2_gnn_in['Wsc0'], 'L2_gnn_Wsc1': _L2_gnn_in['Wsc1'], 'L2_gnn_Wl1_0': _L2_gnn_in['Wl1_0'], 'L2_gnn_Wl1_1': _L2_gnn_in['Wl1_1'], 'L2_gnn_Wl2_s': _L2_gnn_in['Wl2_s'], 'L2_gnn_Wl2_v': _L2_gnn_in['Wl2_v'], 'L2_gnn_Wa': _L2_gnn_in['Wa'], 'L3_gnn_Ws_sc_a': _L3_gnn_in['Ws_sc_a'], 'L3_gnn_Wv_sc_a': _L3_gnn_in['Wv_sc_a'], 'L3_gnn_Ws_sc_c': _L3_gnn_in['Ws_sc_c'], 'L3_gnn_Wv_sc_c': _L3_gnn_in['Wv_sc_c'], 'L3_gnn_Ws_l1_a': _L3_gnn_in['Ws_l1_a'], 'L3_gnn_Wv_l1_a': _L3_gnn_in['Wv_l1_a'], 'L3_gnn_Ws_l1_c': _L3_gnn_in['Ws_l1_c'], 'L3_gnn_Wv_l1_c': _L3_gnn_in['Wv_l1_c'], 'L3_gnn_W_fc1': _L3_gnn_in['W_fc1'], 'L3_gnn_W_fc2': _L3_gnn_in['W_fc2'], 'L3_gnn_Ws_l2_a': _L3_gnn_in['Ws_l2_a'], 'L3_gnn_Wv_l2_a': _L3_gnn_in['Wv_l2_a'], 'L3_gnn_Ws_l2_c': _L3_gnn_in['Ws_l2_c'], 'L3_gnn_Wv_l2_c': _L3_gnn_in['Wv_l2_c'], 'L3_gnn_Ws_l3': _L3_gnn_in['Ws_l3'], 'L3_gnn_Wv_l3': _L3_gnn_in['Wv_l3']}

def reference(x, src, dst, edge_attr_10, edge_attr_16, edge_attr_4, edge_attr_8, node_vec1, node_vec1_n2, node_vec1_n3, L0_gnn_W_sc_s, L0_gnn_W_sc_v, L0_gnn_W1_s, L0_gnn_W1_v, L0_gnn_W2_s, L0_gnn_W2_v, L0_gnn_W3, L0_gnn_fcW1, L0_gnn_fcW2, L1_gnn_W_si0, L1_gnn_W_si1, L1_gnn_W_l1_0, L1_gnn_W_l1_1, L1_gnn_W_l2_00, L1_gnn_W_l2_10, L1_gnn_W_l2_01, L1_gnn_W_l2_11, L1_gnn_W_fc1, L1_gnn_W_fc2, L2_gnn_Wfc1, L2_gnn_Wfc2, L2_gnn_Wsc0, L2_gnn_Wsc1, L2_gnn_Wl1_0, L2_gnn_Wl1_1, L2_gnn_Wl2_s, L2_gnn_Wl2_v, L2_gnn_Wa, L3_gnn_Ws_sc_a, L3_gnn_Wv_sc_a, L3_gnn_Ws_sc_c, L3_gnn_Wv_sc_c, L3_gnn_Ws_l1_a, L3_gnn_Wv_l1_a, L3_gnn_Ws_l1_c, L3_gnn_Wv_l1_c, L3_gnn_W_fc1, L3_gnn_W_fc2, L3_gnn_Ws_l2_a, L3_gnn_Wv_l2_a, L3_gnn_Ws_l2_c, L3_gnn_Wv_l2_c, L3_gnn_Ws_l3, L3_gnn_Wv_l3):
    import jax
    import jax.numpy as jnp

    def _L0_gnn_ref(node_input, node_attr, edge_attr, edge_scalars, W_sc_s, W_sc_v, W1_s, W1_v, W2_s, W2_v, W3, fcW1, fcW2, edge_src, edge_dst):
        import jax, jax.numpy as jnp
        import numpy as np
        N = 625
        E = 6250
        MUL0, MUL1 = (64, 32)
        RAD, HID = (8, 64)
        WNUM = 192
        NUM_NEIGHBORS = 10.0
        INV3 = 1.0 / np.sqrt(3.0)

        def _lin(s, v, Ws, Wv, attr):
            out_s = s @ Ws * attr * (1.0 / np.sqrt(Ws.shape[0]))
            out_v = jnp.einsum('nud,uv->nvd', v, Wv) * attr[..., None] * (1.0 / np.sqrt(Wv.shape[0]))
            return (out_s, out_v)
        n = node_input.shape[0]
        s_in = node_input[:, :MUL0]
        v_in = node_input[:, MUL0:].reshape(n, MUL1, 3)
        sc_s, sc_v = _lin(s_in, v_in, W_sc_s, W_sc_v, node_attr)
        f_s, f_v = _lin(s_in, v_in, W1_s, W1_v, node_attr)
        h = jax.nn.silu(edge_scalars @ fcW1 * (1.0 / np.sqrt(RAD)))
        w = h @ fcW2 * (1.0 / np.sqrt(HID))
        wA, wB, wC, wD = (w[:, :64], w[:, 64:128], w[:, 128:160], w[:, 160:192])
        xs = f_s[edge_src]
        xv = f_v[edge_src]
        y0 = edge_attr[:, :1]
        y1 = edge_attr[:, 1:4]
        outA = wA * xs * y0
        outD = wD * jnp.einsum('eud,ed->eu', xv, y1) * INV3
        outB = wB[:, :, None] * xs[:, :, None] * y1[:, None, :]
        outC = wC[:, :, None] * xv * y0[:, :, None]
        edge_feat = jnp.concatenate([outA, outD, outB.reshape(-1, MUL0 * 3), outC.reshape(-1, MUL1 * 3)], axis=1)
        agg = jax.ops.segment_sum(edge_feat, edge_dst, num_segments=n)
        agg = agg * (1.0 / np.sqrt(NUM_NEIGHBORS))
        ms = agg[:, :MUL0 + MUL1]
        mv = agg[:, MUL0 + MUL1:].reshape(n, MUL0 + MUL1, 3)
        c_s, c_v = _lin(ms, mv, W2_s, W2_v, node_attr)
        conv = jnp.concatenate([c_s, c_v.reshape(n, -1)], axis=1)
        sc = jnp.concatenate([sc_s, sc_v.reshape(n, -1)], axis=1)
        angle = 0.1 * (ms @ W3) * node_attr * (1.0 / np.sqrt(MUL0 + MUL1))
        cos, sin = (jnp.cos(angle), jnp.sin(angle))
        return cos * sc + sin * conv

    def _L1_gnn_ref(node_input, node_attr, edge_src, edge_dst, edge_attr, edge_length_embedded, W_si0, W_si1, W_l1_0, W_l1_1, W_l2_00, W_l2_10, W_l2_01, W_l2_11, W_fc1, W_fc2):
        import jax, jax.numpy as jnp
        import numpy as np
        N_NODES = 50000
        N_EDGES = 12500
        MUL0, MUL1 = (64, 32)
        N_BASIS, N_RADIAL = (10, 100)
        W_NUMEL = 192
        NUM_NEIGHBORS = 16.0
        INV_SQRT3 = np.float32(1.0 / np.sqrt(3.0))
        RELU_GAIN = np.float32(np.sqrt(2.0))
        FAN_L2 = np.float32(np.sqrt(MUL0 + MUL1))

        def _fctp_scalar_attr(x0, x1, a, W0, W1):
            o0 = x0 @ W0 * a * (1.0 / np.sqrt(W0.shape[0]))
            o1 = jnp.einsum('nud,uw->nwd', x1, W1) * a[..., None] * (1.0 / np.sqrt(W1.shape[0]))
            return (o0, o1)
        N = node_input.shape[0]
        x0 = node_input[:, :MUL0]
        x1 = node_input[:, MUL0:].reshape(N, MUL1, 3)
        a = node_attr
        h = jax.nn.relu(edge_length_embedded @ W_fc1 * (1.0 / np.sqrt(N_BASIS))) * RELU_GAIN
        w = h @ W_fc2 * (1.0 / np.sqrt(N_RADIAL))
        w0, w1, w2, w3 = (w[:, :64], w[:, 64:128], w[:, 128:160], w[:, 160:192])
        si0, si1 = _fctp_scalar_attr(x0, x1, a, W_si0, W_si1)
        l0, l1 = _fctp_scalar_attr(x0, x1, a, W_l1_0, W_l1_1)
        y0 = l0[edge_src]
        y1 = l1[edge_src]
        e0 = edge_attr[:, :1]
        e1 = edge_attr[:, 1:4]
        m0 = w0 * y0 * e0
        m1 = (w1 * y0)[:, :, None] * e1[:, None, :]
        m2 = (w2 * e0)[:, :, None] * y1
        m3 = w3 * jnp.einsum('eud,ed->eu', y1, e1) * INV_SQRT3
        inv = np.float32(1.0 / np.sqrt(NUM_NEIGHBORS))
        s0 = jax.ops.segment_sum(m0, edge_dst, num_segments=N) * inv
        s1 = jax.ops.segment_sum(m1, edge_dst, num_segments=N) * inv
        s2 = jax.ops.segment_sum(m2, edge_dst, num_segments=N) * inv
        s3 = jax.ops.segment_sum(m3, edge_dst, num_segments=N) * inv
        o0 = (s0 @ W_l2_00 + s3 @ W_l2_10) * a / FAN_L2
        o1 = (jnp.einsum('nud,uw->nwd', s1, W_l2_01) + jnp.einsum('nud,uw->nwd', s2, W_l2_11)) * a[..., None] / FAN_L2
        out0 = si0 + 0.5 * o0
        out1 = si1 + 0.5 * o1
        return jnp.concatenate([out0, out1.reshape(N, 3 * MUL1)], axis=1)

    def _L2_gnn_ref(x, node_attr, edge_scalars, edge_attr_sh, edge_src, edge_dst, Wfc1, Wfc2, Wsc0, Wsc1, Wl1_0, Wl1_1, Wl2_s, Wl2_v, Wa):
        import jax, jax.numpy as jnp
        import numpy as np
        N = 20000
        E = 5000
        MUL0 = 64
        MUL1 = 32
        FC_IN = 16
        FC_H = 64
        WNUM = 192
        n = x.shape[0]
        x0 = x[:, :MUL0]
        x1 = x[:, MUL0:].reshape(n, MUL1, 3)
        a = node_attr
        h = jax.nn.silu(edge_scalars @ (Wfc1 / jnp.sqrt(jnp.float32(FC_IN))))
        w = h @ (Wfc2 / jnp.sqrt(jnp.float32(FC_H)))
        w0 = w[:, :64]
        w1 = w[:, 64:128]
        w2 = w[:, 128:160]
        w3 = w[:, 160:192]
        inv8 = 1.0 / jnp.sqrt(jnp.float32(MUL0))
        inv32 = 1.0 / jnp.sqrt(jnp.float32(MUL1))
        sc = jnp.concatenate([x0 @ Wsc0 * a * inv8, (jnp.einsum('num,uv->nvm', x1, Wsc1) * a[..., None] * inv32).reshape(n, 3 * MUL1)], axis=1)
        f0 = x0 @ Wl1_0 * a * inv8
        f1 = jnp.einsum('num,uv->nvm', x1, Wl1_1) * a[..., None] * inv32
        e0 = f0[edge_src]
        e1 = f1[edge_src]
        sh0 = edge_attr_sh[:, :1]
        sh1 = edge_attr_sh[:, 1:4]
        mid0 = w0 * e0 * sh0
        mid1 = w3 * jnp.einsum('eum,em->eu', e1, sh1) / jnp.sqrt(3.0)
        mid2 = w1[:, :, None] * e0[:, :, None] * sh1[:, None, :]
        mid3 = w2[:, :, None] * e1 * sh0[:, :, None]
        cnt = jnp.clip(jax.ops.segment_sum(jnp.ones(edge_dst.shape, x.dtype), edge_dst, num_segments=n), 1.0)

        def smean(v):
            s = jax.ops.segment_sum(v, edge_dst, num_segments=n)
            return s / cnt.reshape((n,) + (1,) * (v.ndim - 1))
        n0, n1 = (smean(mid0), smean(mid1))
        n2, n3 = (smean(mid2), smean(mid3))
        scal = jnp.concatenate([n0, n1], axis=1)
        vec = jnp.concatenate([n2, n3], axis=1)
        inv96 = 1.0 / jnp.sqrt(jnp.float32(MUL0 + MUL1))
        alpha = scal @ Wa * a * inv96
        out_s = scal @ Wl2_s * a * inv96
        out_v = jnp.einsum('num,uv->nvm', vec, Wl2_v) * a[..., None] * inv96
        conv = jnp.concatenate([out_s, out_v.reshape(n, 3 * MUL1)], axis=1)
        return sc + alpha * conv

    def _L3_gnn_ref(node_input, node_attr, node_crystal_attr, sym_mask, edge_attr, edge_length_embedded, edge_src, edge_dst, Ws_sc_a, Wv_sc_a, Ws_sc_c, Wv_sc_c, Ws_l1_a, Wv_l1_a, Ws_l1_c, Wv_l1_c, W_fc1, W_fc2, Ws_l2_a, Wv_l2_a, Ws_l2_c, Wv_l2_c, Ws_l3, Wv_l3):
        import jax, jax.numpy as jnp
        import numpy as np
        N = 25000
        E = 6250
        S = 64
        V = 32
        NB = 10
        H = 100
        WN = 192
        MID = 96
        NUM_NEIGHBORS = 16.0
        C_S = float(np.sin(np.pi / 8.0))
        C_X = float(np.cos(np.pi / 8.0))
        SQRT3 = float(np.sqrt(3.0))

        def fctp_scalar_attr(xs, xv, attr, Ws, Wv):
            s = xs * attr @ Ws
            v = jnp.einsum('nuc,uo->noc', xv * attr[:, :, None], Wv)
            return (s, v)
        n = node_input.shape[0]
        xs = node_input[:, :S]
        xv = node_input[:, S:].reshape(n, V, 3)
        ssa, sva = fctp_scalar_attr(xs, xv, node_attr, Ws_sc_a, Wv_sc_a)
        ssc, svc = fctp_scalar_attr(xs, xv, node_crystal_attr, Ws_sc_c, Wv_sc_c)
        s_s, s_v = (ssa + ssc, sva + svc)
        l1a_s, l1a_v = fctp_scalar_attr(xs, xv, node_attr, Ws_l1_a, Wv_l1_a)
        l1c_s, l1c_v = fctp_scalar_attr(xs, xv, node_crystal_attr, Ws_l1_c, Wv_l1_c)
        x1s, x1v = (l1a_s + l1c_s, l1a_v + l1c_v)
        weight = jax.nn.silu(edge_length_embedded @ W_fc1) @ W_fc2
        w0 = weight[:, :S]
        w1 = weight[:, S:2 * S]
        w2 = weight[:, 2 * S:2 * S + V]
        w3 = weight[:, 2 * S + V:]
        gs = x1s[edge_src]
        gv = x1v[edge_src]
        e_s = edge_attr[:, :1]
        e_v = edge_attr[:, 1:]
        mid0a = w0 * gs * e_s
        mid0b = w3 * (jnp.einsum('euc,ec->eu', gv, e_v) / SQRT3)
        mid1a = w1[:, :, None] * gs[:, :, None] * e_v[:, None, :]
        mid1b = w2[:, :, None] * gv * e_s[:, :, None]
        edge_feat = jnp.concatenate([mid0a, mid0b, mid1a.reshape(-1, 3 * S), mid1b.reshape(-1, 3 * V)], axis=-1)
        agg = jax.ops.segment_sum(edge_feat, edge_dst, num_segments=n) / np.sqrt(NUM_NEIGHBORS)
        m_s = agg[:, :MID]
        m_v = agg[:, MID:].reshape(n, MID, 3)
        l2a_s, l2a_v = fctp_scalar_attr(m_s, m_v, node_attr, Ws_l2_a, Wv_l2_a)
        l2c_s, l2c_v = fctp_scalar_attr(m_s, m_v, node_crystal_attr, Ws_l2_c, Wv_l2_c)
        m_s, m_v = (l2a_s + l2c_s, l2a_v + l2c_v)
        o_s, o_v = fctp_scalar_attr(m_s, m_v, sym_mask, Ws_l3, Wv_l3)
        out_s = C_S * s_s + C_X * o_s
        out_v = C_S * s_v + C_X * o_v
        return jnp.concatenate([out_s, out_v.reshape(n, 3 * V)], axis=-1)
    x = _layernorm(x + _L0_gnn_ref(x, node_vec1, edge_attr_4, edge_attr_8, L0_gnn_W_sc_s, L0_gnn_W_sc_v, L0_gnn_W1_s, L0_gnn_W1_v, L0_gnn_W2_s, L0_gnn_W2_v, L0_gnn_W3, L0_gnn_fcW1, L0_gnn_fcW2, src, dst), axis=-1)
    x = _layernorm(x + _L1_gnn_ref(x, node_vec1, src, dst, edge_attr_4, edge_attr_10, L1_gnn_W_si0, L1_gnn_W_si1, L1_gnn_W_l1_0, L1_gnn_W_l1_1, L1_gnn_W_l2_00, L1_gnn_W_l2_10, L1_gnn_W_l2_01, L1_gnn_W_l2_11, L1_gnn_W_fc1, L1_gnn_W_fc2), axis=-1)
    x = _layernorm(x + _L2_gnn_ref(x, node_vec1, edge_attr_16, edge_attr_4, src, dst, L2_gnn_Wfc1, L2_gnn_Wfc2, L2_gnn_Wsc0, L2_gnn_Wsc1, L2_gnn_Wl1_0, L2_gnn_Wl1_1, L2_gnn_Wl2_s, L2_gnn_Wl2_v, L2_gnn_Wa), axis=-1)
    x = _layernorm(x + _L3_gnn_ref(x, node_vec1, node_vec1_n2, node_vec1_n3, edge_attr_4, edge_attr_10, src, dst, L3_gnn_Ws_sc_a, L3_gnn_Wv_sc_a, L3_gnn_Ws_sc_c, L3_gnn_Wv_sc_c, L3_gnn_Ws_l1_a, L3_gnn_Wv_l1_a, L3_gnn_Ws_l1_c, L3_gnn_Wv_l1_c, L3_gnn_W_fc1, L3_gnn_W_fc2, L3_gnn_Ws_l2_a, L3_gnn_Wv_l2_a, L3_gnn_Ws_l2_c, L3_gnn_Wv_l2_c, L3_gnn_Ws_l3, L3_gnn_Wv_l3), axis=-1)
    return x

_drawn_inputs = setup_inputs


def setup_inputs(seed=0):
    import zlib

    import numpy as np

    out = dict(_drawn_inputs(seed))
    spreads = {}
    factors = {'edge_attr_10': 5.24,
     'edge_attr_16': 8.0,
     'edge_attr_8': 8.0,
     'node_vec1_n3': 5.553,
     'L0_gnn_W1_s': 8.0,
     'L0_gnn_W1_v': 8.0,
     'L0_gnn_W2_s': 8.0,
     'L0_gnn_W2_v': 8.0,
     'L0_gnn_W3': 8.0,
     'L0_gnn_fcW1': 8.0,
     'L0_gnn_fcW2': 8.0,
     'L1_gnn_W_l1_0': 6.088,
     'L1_gnn_W_l1_1': 8.0,
     'L1_gnn_W_l2_00': 8.0,
     'L1_gnn_W_l2_10': 8.0,
     'L1_gnn_W_l2_01': 7.329,
     'L1_gnn_W_l2_11': 8.0,
     'L1_gnn_W_fc1': 6.257,
     'L1_gnn_W_fc2': 5.392,
     'L2_gnn_Wfc1': 8.0,
     'L2_gnn_Wfc2': 8.0,
     'L2_gnn_Wl1_0': 8.0,
     'L2_gnn_Wl1_1': 8.0,
     'L2_gnn_Wl2_s': 8.0,
     'L2_gnn_Wl2_v': 8.0,
     'L2_gnn_Wa': 8.0,
     'L3_gnn_Ws_l1_a': 5.057,
     'L3_gnn_Wv_l1_a': 6.44,
     'L3_gnn_Ws_l1_c': 4.942,
     'L3_gnn_Wv_l1_c': 6.618,
     'L3_gnn_W_fc1': 3.234,
     'L3_gnn_W_fc2': 2.846,
     'L3_gnn_Ws_l2_a': 6.378,
     'L3_gnn_Wv_l2_a': 4.991,
     'L3_gnn_Ws_l2_c': 6.437,
     'L3_gnn_Wv_l2_c': 4.922,
     'L3_gnn_Ws_l3': 4.386,
     'L3_gnn_Wv_l3': 3.599}
    for name, (base, spread) in spreads.items():
        noise = np.random.default_rng([zlib.crc32(name.encode()), seed]).standard_normal(out[name].shape)
        drawn = base * np.exp(spread * noise) if base else spread * noise
        out[name] = jnp.asarray(drawn.astype(out[name].dtype))
    for name, factor in factors.items():
        out[name] = (out[name] * factor).astype(out[name].dtype)
    return out
```

```python
import numpy as np
import concourse.bass as bass
from concourse import mybir
from contextlib import ExitStack

N_NODES, N_EDGES = 50000, 25000
S, V = 64, 32
F = S + 3 * V
XW = F + 4
P = 128
BT = 4
NBLK = 100
NP = NBLK * BT * P
NPAIR = 98
NT = 2 * NPAIR
EP = NT * P
EA = 38
RING = 4
AW = 2 + F
AW3 = 2 * F
XC = 192
MR = 2 + S + V
FAR = 262144.0
R3 = float(1.0 / np.sqrt(3.0))
C_S, C_X = float(np.sin(np.pi / 8.0)), float(np.cos(np.pi / 8.0))
EPS = 1e-5
SORT_COLS = 784
TWO_PI_HI = 6.28125
TWO_PI_LO = float(2 * np.pi - 6.28125)
ROUND = 12582912.0

r = lambda n: float(1.0 / np.sqrt(float(n)))
LAYERS = [
    dict(rad=8, at=4, hid=64, silu=True, hs=r(8), w=r(64), fs=r(64), fv=r(32), sc=r(64), scv=r(32),
         conv=r(10) * r(96), extra=0.1 * r(10) * r(96), groups=1),
    dict(rad=10, at=12, hid=100, silu=False, hs=r(10), w=float(np.sqrt(2.0)) * r(100), fs=r(64), fv=r(32),
         sc=r(64), scv=r(32), conv=0.5 * 0.25 * r(96), extra=1.0, groups=1),
    dict(rad=16, at=22, hid=64, silu=True, hs=r(16), w=r(64), fs=r(64), fv=r(32), sc=r(64), scv=r(32),
         conv=r(96), extra=r(96), groups=1),
    dict(rad=10, at=12, hid=100, silu=True, hs=1.0, w=1.0, fs=1.0, fv=1.0, sc=C_S, scv=C_S,
         conv=C_X * 0.25, extra=1.0, groups=2),
]

WEIGHTS = ['L0_gnn_W_sc_s', 'L0_gnn_W_sc_v', 'L0_gnn_W1_s', 'L0_gnn_W1_v', 'L0_gnn_W2_s', 'L0_gnn_W2_v',
           'L0_gnn_W3', 'L0_gnn_fcW1', 'L0_gnn_fcW2', 'L1_gnn_W_si0', 'L1_gnn_W_si1', 'L1_gnn_W_l1_0',
           'L1_gnn_W_l1_1', 'L1_gnn_W_l2_00', 'L1_gnn_W_l2_10', 'L1_gnn_W_l2_01', 'L1_gnn_W_l2_11',
           'L1_gnn_W_fc1', 'L1_gnn_W_fc2', 'L2_gnn_Wfc1', 'L2_gnn_Wfc2', 'L2_gnn_Wsc0', 'L2_gnn_Wsc1',
           'L2_gnn_Wl1_0', 'L2_gnn_Wl1_1', 'L2_gnn_Wl2_s', 'L2_gnn_Wl2_v', 'L2_gnn_Wa', 'L3_gnn_Ws_sc_a',
           'L3_gnn_Wv_sc_a', 'L3_gnn_Ws_sc_c', 'L3_gnn_Wv_sc_c', 'L3_gnn_Ws_l1_a', 'L3_gnn_Wv_l1_a',
           'L3_gnn_Ws_l1_c', 'L3_gnn_Wv_l1_c', 'L3_gnn_W_fc1', 'L3_gnn_W_fc2', 'L3_gnn_Ws_l2_a',
           'L3_gnn_Wv_l2_a', 'L3_gnn_Ws_l2_c', 'L3_gnn_Wv_l2_c', 'L3_gnn_Ws_l3', 'L3_gnn_Wv_l3']


def back(k, turn, lag):
    return (k - lag) % RING, turn + (k - lag) // RING


def steps(eng, first, last, steady, body):
    lo, hi = steady
    for q in range(first, lo):
        body(q, q % RING, q // RING)
    with eng.Fori(0, (hi - lo) // RING) as i:
        for k in range(RING):
            body(i * RING + (lo + k), k, i + lo // RING)
    for q in range(hi, last):
        body(q, q % RING, q // RING)


def within(q, lo, hi):
    return lo <= q < hi if isinstance(q, int) else True


def wait(eng, sem, value):
    if isinstance(value, int) and value <= 0:
        return
    eng.wait_ge(sem, value)


def alone(eng, passed):
    eng.sem_inc(passed, 1)


def build(nc, nodes, pairs, eattr, w, out):
    f32, i32 = mybir.dt.float32, mybir.dt.int32
    ALU, ACT, AX = mybir.AluOpType, mybir.ActivationFunctionType, mybir.AxisListType
    ctx = ExitStack()
    with ctx:
        def sb(name, shape, dt=f32):
            return ctx.enter_context(nc.sbuf_tensor(name, shape, dt))

        def sem(name):
            return ctx.enter_context(nc.semaphore(name))

        def sems(name, n):
            return [sem(f"{name}{i}") for i in range(n)]

        xtab = [nodes] + [nc.dram_tensor(f"x_after_{l}", (NP, XW), f32, kind="Internal").ap() for l in range(3)]
        agg = nc.dram_tensor("aggregates", (NP, AW), f32, kind="Internal").ap()
        agg3 = nc.dram_tensor("aggregates_3", (NP, AW3), f32, kind="Internal").ap()
        rec_pairs = nc.dram_tensor("sorted_pairs", (EP, 2), i32, kind="Internal").ap()
        rec_attr = nc.dram_tensor("sorted_attr", (EP, EA), f32, kind="Internal").ap()
        dst_row = nc.dram_tensor("sorted_dst", (1, EP), f32, kind="Internal").ap()
        dst_row0 = nc.dram_tensor("given_dst", (1, EP), f32, kind="Internal").ap()

        same_all = sb("same_all", [P, EP])
        meta_all = sb("meta_all", [P, NPAIR, 16])
        dst_col = sb("dst_col", [P, NPAIR, 2])
        ident = sb("ident", [P, P])
        ones = sb("ones", [P, 1])
        eps = sb("eps", [P, 1])
        zeros = sb("zeros", [P, 2025])
        fc1 = [sb(f"fc1_{l}", [P, L["hid"]]) for l, L in enumerate(LAYERS)]
        fc2 = [sb(f"fc2_{l}", [L["hid"], 192]) for l, L in enumerate(LAYERS)]
        w1s = [sb(f"w1s_{l}", [S, L["groups"] * S]) for l, L in enumerate(LAYERS)]
        w1v = [sb(f"w1v_{l}", [96, L["groups"] * 96]) for l, L in enumerate(LAYERS)]
        scs = [sb(f"scs_{l}", [S, L["groups"] * S]) for l, L in enumerate(LAYERS)]
        scv = [sb(f"scv_{l}", [96, L["groups"] * 96]) for l, L in enumerate(LAYERS)]
        aw = [AW, AW, AW, AW3]
        w2 = [sb(f"w2_{l}", [MR, 2, aw[l]]) for l in range(4)]

        meta = sb("meta", [P, RING, 16])
        sidx = sb("sidx", [P, RING, 2])
        xg = sb("xg", [P, RING, 2, XC])
        xT = sb("xT", [P, 2, 512])
        hT = sb("hT", [100, 2, 256])
        yv = sb("yv", [P, 2, 2, 4])
        wy = sb("wy", [P, 2, 2, 4, 96])
        msg = sb("msg", [P, 2, 2, 4, MR])
        dprod = sb("dprod", [P, 2, 3, 32])
        fsum = sb("fsum", [P, 2, 2, F])
        aggT = sb("aggT", [MR, 2, 512])
        tot = sb("tot", [P, RING, 2, AW3])

        arena = sb("arena", [P, RING * BT * (XW + AW + F)])
        o1 = RING * BT * XW
        o2 = o1 + RING * BT * AW
        xn = arena[:, 0:o1].rearrange("p (r t c) -> p r t c", r=RING, t=BT)
        an = arena[:, o1:o2].rearrange("p (r t c) -> p r t c", r=RING, t=BT)
        yn = arena[:, o2:o2 + RING * BT * F].rearrange("p (r t c) -> p r t c", r=RING, t=BT)
        an3 = same_all[:, 0:RING * BT * AW3].rearrange("p (r t c) -> p r t c", r=RING, t=BT)
        stats = sb("stats", [P, 2, BT, 6])
        mv = sb("mv", [P, RING, BT, 2])
        std = sb("std", [P, RING, BT])
        rstd = sb("rstd", [P, RING, BT])
        shift = sb("shift", [P, RING, BT])
        gates = sb("gates", [P, RING, BT, 2])
        trig = sb("trig", [P, RING, 6, 2, BT])
        inv_count = sb("inv_count", [P, RING, 2, BT])

        def part(a, n, rows=NPAIR):
            return arena[0:rows, a:a + n]

        pairs0 = part(0, 512).bitcast(i32)
        prev0 = part(512, 512).bitcast(i32)
        dst0 = part(1024, 256)
        prv0 = part(1280, 256)
        less0 = part(1536, 256)
        viol = part(1792, 1)
        dcol0 = arena[:, 1800:1800 + 2 * NPAIR].rearrange("p (q t) -> p q t", t=2)
        flag = part(1996, 1, 1).bitcast(i32)
        pairs1 = part(2000, 512).bitcast(i32)
        prev1 = part(2512, 512).bitcast(i32)
        next1 = part(3024, 2).bitcast(i32)
        dst1 = part(3028, 256)
        src1 = part(3284, 256)
        prv1 = part(3540, 256)
        nxt1 = part(3796, 1)
        same1 = part(3800, 256)
        idx1 = part(4056, 256)
        carry1 = part(4312, 256)
        sort_iota = arena[:, 4600:4600 + SORT_COLS]
        sort_a = arena[:, 5400:5400 + SORT_COLS]
        sort_b = arena[:, 6200:6200 + SORT_COLS]
        sort_s = arena[:, 7000:7016]
        sort_pair = arena[:, 7020:7022].bitcast(i32)
        sort_attr = arena[:, 7024:7024 + EA]
        attr_rows = same_all[0:NPAIR, 4096:4096 + 256 * EA]
        stage = same_all[:, 0:4096]

        bank = [ctx.enter_context(nc.psum_tensor(f"bank{i}", [P, 512], f32)) for i in range(8)]

        passed = {e: sem(f"passed_{e}") for e in ("sp", "gp", "pe", "dve")}
        filled = sem("filled")
        given_in, given_seen = sem("given_in"), sem("given_seen")
        viol_ready, viol_summed, flag_ready = sem("viol_ready"), sem("viol_summed"), sem("flag_ready")
        dcol_turned = sem("dcol_turned")
        copied, sort_dma, pos_ready, sort_io, sort_chain = (sem("copied"), sem("sort_dma"), sem("pos_ready"),
                                                            sem("sort_io"), sem("sort_chain"))
        ranks_free = sem("ranks_free")
        bcast_in, scattered, iota_ready = sem("bcast_in"), sem("scattered"), sem("iota_ready")
        records_ready = sem("records_ready")
        stage_zero, rows_in, attr_in0, stage_in = sem("stage_zero"), sem("rows_in"), sem("attr_in0"), sem("stage_in")
        ident_ready, ident_a = sem("ident_ready"), sem("ident_a")
        chain = sem("chain")
        fields_ready, fields_turned = sem("fields_ready"), sem("fields_turned")
        l2_turned, l2_copied, l2_product = sem("l2_turned"), sem("l2_copied"), sem("l2_product")
        dst_out, dst_in, weights_ready, same_ready = sem("dst_out"), sem("dst_in"), sem("weights_ready"), sem("same_ready")
        meta_ready = sem("meta_ready")
        CHAIN_DST = 6
        zeroed, zeroed3 = sem("zeroed"), sem("zeroed3")

        meta_in, ea_in, sidx_in = sems("meta_in", RING), sems("ea_in", RING), sems("sidx_in", RING)
        gathered, spread = sems("gathered", RING), sems("spread", RING)
        turned, turned_out = sem("turned"), sem("turned_out")
        h_ready, h_act, f_ready, w_ready = sem("h_ready"), sem("h_act"), sem("f_ready"), sem("w_ready")
        y_ready, wy_ready, dprod_ready, msg_ready = sem("y_ready"), sem("wy_ready"), sem("dprod_ready"), sem("msg_ready")
        fa_out, f_summed = sem("fa_out"), sem("f_summed")
        carried_tot = sem("carried_tot")
        summed, summed_out = sems("summed", 2), sems("summed_out", 2)
        tot_ready, carried, tot_out = sems("tot_ready", 2), sems("carried", 2), sem("tot_out")

        y_half, y_part, count_max = sem("y_half"), sem("y_part"), sem("count_max")
        TRIG_OPS = 12
        PC2 = TRIG_OPS * NBLK
        x_in, a_in, stored = sems("x_in", RING), sems("a_in", RING), sems("stored", RING)
        nturned, nturned_out, sc_ready = sem("nturned"), sem("nturned_out"), sem("sc_ready")
        y_stt, y_sum, stats_ready, mv_ready = sem("y_stt"), sem("y_sum"), sem("stats_ready"), sem("mv_ready")
        std_ready, rstd_ready, shift_ready, normed = sem("std_ready"), sem("rstd_ready"), sem("shift_ready"), sem("normed")
        gates_ready, trig_ready, sin_ready, count_ready, pool_chain = (sem("gates_ready"), sem("trig_ready"),
                                                                       sem("sin_ready"), sem("count_ready"), sem("pool_chain"))

        slot_uses = [len(range(k, NPAIR, RING)) for k in range(RING)]
        EDGE_STEADY, POOL_STEADY = (4, 96), (8, 96)
        NODE_STEADY = (4, NBLK)

        def edge_count(l, q):
            return q + (l * NPAIR + 1)

        def slot_count(l, k, turn):
            return turn + (l * slot_uses[k] + 1)

        def node_count(l, b):
            return b + (l * NBLK + 1)

        def node_slot(l, turn):
            return turn + (l * (NBLK // RING) + 1)

        block = ctx.enter_context(nc.Block())

        N_ROWS_IN, N_STAGE = 5, 0

        def weight_loads():
            g = lambda n: w[n]
            loads = []
            for l, L in enumerate(LAYERS):
                names = [
                    dict(fc1='L0_gnn_fcW1', fc2='L0_gnn_fcW2', s=['L0_gnn_W1_s'], v=['L0_gnn_W1_v'],
                         cs=['L0_gnn_W_sc_s'], cv=['L0_gnn_W_sc_v'], l2s=['L0_gnn_W2_s'], l2v=['L0_gnn_W2_v'],
                         ex='L0_gnn_W3'),
                    dict(fc1='L1_gnn_W_fc1', fc2='L1_gnn_W_fc2', s=['L1_gnn_W_l1_0'], v=['L1_gnn_W_l1_1'],
                         cs=['L1_gnn_W_si0'], cv=['L1_gnn_W_si1'], l2s=['L1_gnn_W_l2_00', 'L1_gnn_W_l2_10'],
                         l2v=['L1_gnn_W_l2_01', 'L1_gnn_W_l2_11'], ex=None),
                    dict(fc1='L2_gnn_Wfc1', fc2='L2_gnn_Wfc2', s=['L2_gnn_Wl1_0'], v=['L2_gnn_Wl1_1'],
                         cs=['L2_gnn_Wsc0'], cv=['L2_gnn_Wsc1'], l2s=['L2_gnn_Wl2_s'], l2v=['L2_gnn_Wl2_v'],
                         ex='L2_gnn_Wa'),
                    dict(fc1='L3_gnn_W_fc1', fc2='L3_gnn_W_fc2', s=['L3_gnn_Ws_l1_a', 'L3_gnn_Ws_l1_c'],
                         v=['L3_gnn_Wv_l1_a', 'L3_gnn_Wv_l1_c'], cs=['L3_gnn_Ws_sc_a', 'L3_gnn_Ws_sc_c'],
                         cv=['L3_gnn_Wv_sc_a', 'L3_gnn_Wv_sc_c'], l2s=None, l2v=None, ex=None),
                ][l]
                st = STAGE[l]
                loads.append((fc1[l][100:100 + L["rad"], :], g(names['fc1'])))
                o, f = st['fc2'], g(names['fc2'])
                for at, a, b in ((0, 0, 64), (64, 128, 160), (96, 64, 128), (160, 160, 192)):
                    loads.append((stage[0:L["hid"], o + at:o + at + b - a], f[:, a:b]))
                for key, name in (('w1s', 's'), ('scs', 'cs')):
                    for j, n in enumerate(names[name]):
                        loads.append((stage[0:S, st[key] + j * S:st[key] + (j + 1) * S], g(n)))
                for key, name in (('w1v', 'v'), ('scv', 'cv')):
                    for j, n in enumerate(names[name]):
                        for d in range(3):
                            c = st[key] + j * 96 + d * V
                            loads.append((stage[d:d + 3 * (V - 1) + 1:3, c:c + V], g(n)))
                if l < 3:
                    o, row = st['w2'], 1
                    for n in names['l2s']:
                        loads.append((stage[row:row + g(n).shape[0], o + 2:o + 2 + S], g(n)))
                        row += g(n).shape[0]
                    row = 1
                    for n in names['l2v']:
                        for d in range(3):
                            c = o + 2 + S + d * V
                            loads.append((stage[row:row + g(n).shape[0], c:c + V], g(n)))
                        row += g(n).shape[0]
                    if names['ex']:
                        loads.append((stage[1:97, o:o + 1], g(names['ex'])))
                    if l == 2:
                        loads.append((stage[97:98, o + 1:o + 2], ones[0:1, 0:1]))
                else:
                    o = st['l2']
                    for j, n in enumerate(('L3_gnn_Ws_l2_a', 'L3_gnn_Ws_l2_c', 'L3_gnn_Wv_l2_a', 'L3_gnn_Wv_l2_c')):
                        loads.append((stage[0:96, o + 96 * j:o + 96 * j + 96], g(n)))
                    loads.append((stage[0:96, o + 384:o + 448], g('L3_gnn_Ws_l3')))
                    loads.append((stage[0:96, o + 448:o + 480], g('L3_gnn_Wv_l3')))
            return loads

        STAGE, col = [], 0
        for l, L in enumerate(LAYERS):
            st = {}
            for key, width in (('fc2', 192), ('w1s', L["groups"] * S), ('w1v', L["groups"] * 96),
                               ('scs', L["groups"] * S), ('scv', L["groups"] * 96),
                               ('w2', AW) if l < 3 else ('l2', 480 + 4 * MR)):
                st[key] = col
                col += width
            STAGE.append(st)
        assert col <= 4096
        LOADS = weight_loads()
        flat = lambda ap: ap.rearrange("e c -> (e c)")
        pair_rows = lambda ap: ap.rearrange("(q e) c -> q (e c)", q=NPAIR)

        def edge_rows_before(ap):
            return flat(ap)[510:510 + 512 * (NPAIR - 1)].rearrange("(q c) -> q c", c=512)

        @block.sync
        def _(sp):
            sp.dma_start(pairs0, pair_rows(pairs)).then_inc(given_in, 16)
            sp.wait_ge(filled, 1)
            sp.dma_start(prev0[1:NPAIR, :], edge_rows_before(pairs)).then_inc(given_in, 16)
            sp.dma_start(prev0[0:1, 2:512], pair_rows(pairs)[0:1, 0:510]).then_inc(given_in, 16)
            zrows = flat(agg).rearrange("(c p n) -> c p n", p=P, n=2025)
            for c in range(NP * AW // (P * 2025)):
                sp.dma_start(zrows[c], zeros[:, :]).then_inc(zeroed, 16)
            sp.wait_ge(records_ready, 1)
            sp.wait_ge(stage_zero, 1)
            sp.dma_start(pairs1, pair_rows(rec_pairs)).then_inc(rows_in, 16)
            sp.dma_start(prev1[1:NPAIR, :], edge_rows_before(rec_pairs)).then_inc(rows_in, 16)
            sp.dma_start(prev1[0:1, 2:512], pair_rows(rec_pairs)[0:1, 0:510]).then_inc(rows_in, 16)
            sp.dma_start(next1[0:NPAIR - 1, :], pair_rows(rec_pairs)[1:NPAIR, 0:2]).then_inc(rows_in, 16)
            sp.dma_start(attr_rows, pair_rows(rec_attr)).then_inc(attr_in0, 16)
            with nc.allow_non_contiguous_dma(reason="one column of weights"):
                for to, of in LOADS:
                    sp.dma_start(to, of).then_inc(stage_in, 16)
            sp.wait_ge(chain, CHAIN_DST)
            sp.dma_start(dst_row.rearrange("o (q e) -> (o q) e", q=NPAIR), dst1).then_inc(dst_out, 16)
            sp.wait_ge(dst_out, 16)
            sp.wait_ge(meta_ready, 1)
            sp.wait_ge(weights_ready, 1)
            for c in range(3, -1, -1):
                n = EP // 4
                sp.dma_start(same_all[:, c * n:(c + 1) * n],
                             dst_row[:, c * n:(c + 1) * n].to_broadcast([P, n])).then_inc(dst_in, 16)

            for l in range(4):
                L = LAYERS[l]

                def edge_loads(q, k, turn):
                    if within(q, 0, NPAIR):
                        pair = (NPAIR - 1) - q
                        if not isinstance(q, int):
                            pair = sp.snap(pair)
                        ea = rec_attr.rearrange("(q t p) c -> p q t c", t=2, p=P)
                        wait(sp, msg_ready, edge_count(l, q - RING))
                        alone(sp, passed["sp"])
                        sp.dma_start(meta[:, k, :], meta_all[:, bass.ds(pair, 1), :]
                                     .rearrange("p o c -> p (o c)")).then_inc(meta_in[k], 16)
                        sp.dma_start(xg[:, k, :, XW:XW + L["rad"]],
                                     ea[:, bass.ds(pair, 1), :, L["at"]:L["at"] + L["rad"]]
                                     .rearrange("p o t c -> p (o t) c")).then_inc(ea_in[k], 16)
                    if within(q, 4, NPAIR + 4):
                        pair = (NPAIR + 3) - q
                        if not isinstance(q, int):
                            pair = sp.snap(pair)
                        if l or within(q, 8, NPAIR + 8):
                            kk, tt = back(k, turn, 8)
                            wait(sp, spread[kk], slot_count(l, kk, tt) * 32)
                            alone(sp, passed["sp"])
                        sp.dma_start(sidx[:, k, :], meta_all[:, bass.ds(pair, 1), 2:4]
                                     .rearrange("p o c -> p (o c)")).then_inc(sidx_in[k], 16)

                if l == 0:
                    sp.wait_ge(meta_ready, 1)
                steps(sp, 0, NPAIR + 4, POOL_STEADY, edge_loads)
                if l == 0:
                    z3 = flat(agg3).rearrange("(c p n) -> c p n", p=P, n=2000)
                    for c in range(NP * AW3 // (P * 2000)):
                        sp.dma_start(z3[c], zeros[:, 0:2000]).then_inc(zeroed3, 16)

                xrows = xtab[l].rearrange("(b p t) c -> b p (t c)", p=P, t=BT)
                arows = (agg if l < 3 else agg3).rearrange("(b p t) c -> b p (t c)", p=P, t=BT)
                abuf = an if l < 3 else an3
                for k in range(RING):
                    sp.wait_ge(spread[k], 32 * slot_uses[k] * (l + 1))

                def node_loads(b, k, turn):
                    if not isinstance(b, int):
                        b = sp.snap(b)
                    wait(sp, stored[k], node_slot(l, turn - 1) * 16)
                    alone(sp, passed["sp"])
                    sp.dma_start(xn[:, k].rearrange("p t c -> p (t c)"),
                                 xrows[bass.ds(b, 1)].rearrange("o p c -> (o p) c")).then_inc(x_in[k], 16)
                    sp.dma_start(abuf[:, k].rearrange("p t c -> p (t c)"),
                                 arows[bass.ds(b, 1)].rearrange("o p c -> (o p) c")).then_inc(a_in[k], 16)

                steps(sp, 0, NBLK, NODE_STEADY, node_loads)
            for k in range(RING):
                sp.wait_ge(stored[k], 16 * 4 * (NBLK // RING))
            for c in (zeroed3,):
                sp.wait_ge(c, 16 * (NP * AW3 // (P * 2000)))

        @block.gpsimd
        def _(gp):
            gp.memset(ident[:, :], 0.0).then_inc(ident_a, 1)
            gp.wait_ge(ident_a, 1)
            gp.affine_select(out=ident[:, :], in_=ident[:, :], compare_op=ALU.not_equal, fill=1.0, base=0,
                             pattern=[[-1, P]], channel_multiplier=1).then_inc(ident_ready, 1)
            gp.dma_start(rec_pairs.rearrange("(q e) c -> q (e c)", q=P), pairs.rearrange("(q e) c -> q (e c)", q=P)).then_inc(copied, 16)
            gp.dma_start(rec_attr.rearrange("(q e) c -> q (e c)", q=P), eattr.rearrange("(q e) c -> q (e c)", q=P)).then_inc(copied, 16)
            gp.wait_ge(copied, 32)
            gp.wait_ge(flag_ready, 1)
            unsorted = gp.value_load(flag, min_val=0, max_val=1)
            with gp.If(unsorted > 0):
                gp.iota(sort_a.bitcast(i32), pattern=[[1, SORT_COLS]], base=0, channel_multiplier=0).then_inc(iota_ready, 1)
                gp.iota(sort_s[:, 0:1].bitcast(i32), pattern=[[0, 1]], base=0, channel_multiplier=1).then_inc(iota_ready, 1)
                gp.dma_start(dst_row0.rearrange("o (q e) -> (o q) e", q=NPAIR), dst0).then_inc(sort_dma, 16)
                gp.wait_ge(sort_dma, 16)
                gp.dma_start(same_all[:, :].rearrange("p (a n) -> p a n", n=EP // 4),
                             dst_row0.rearrange("o (a n) -> o a n", n=EP // 4).to_broadcast([P, 4, EP // 4])).then_inc(bcast_in, 16)
                gp.sem_inc(ranks_free, 1)
                with gp.Fori(0, NT) as t:
                    gp.dma_start(sort_pair, pairs[bass.ds(t * P, P), :]).then_inc(sort_io, 16)
                    gp.dma_start(sort_attr, eattr[bass.ds(t * P, P), :]).then_inc(sort_io, 16)
                    gp.wait_ge(sort_io, t * 32 + 32)
                    gp.wait_ge(pos_ready, t + 1)
                    alone(gp, passed["gp"])
                    at = bass.IndirectOffsetOnAxis(ap=sort_s[:, 8:9].bitcast(i32), axis=0)
                    gp.indirect_dma_start(rec_pairs, at, sort_pair, None).then_inc(scattered, 16)
                    gp.indirect_dma_start(rec_attr, at, sort_attr, None).then_inc(scattered, 16)
                    gp.wait_ge(scattered, t * 32 + 32)
                    gp.sem_inc(ranks_free, 1)
            gp.engine_nop().then_inc(records_ready, 1)
            gp.wait_ge(meta_ready, 1)
            for l in range(4):
                def edge_moves(q, k, turn):
                    if within(q, 0, NPAIR):
                        gp.wait_ge(meta_in[k], slot_count(l, k, turn) * 16)
                        wait(gp, turned, edge_count(l, q - RING))
                        alone(gp, passed["gp"])
                        for t in range(2):
                            at = bass.IndirectOffsetOnAxis(ap=meta[:, k, t:t + 1].bitcast(i32), axis=0)
                            gp.indirect_dma_start(xg[:, k, t, 0:XW], None, xtab[l], at).then_inc(gathered[k], 16)
                    if within(q, 6, NPAIR + 6):
                        kk, tt = back(k, turn, 6)
                        gp.wait_ge(tot_out, edge_count(l, q - 6))
                        gp.wait_ge(sidx_in[kk], slot_count(l, kk, tt) * 16)
                        alone(gp, passed["gp"])
                        for t in range(2):
                            at = bass.IndirectOffsetOnAxis(ap=sidx[:, kk, t:t + 1].bitcast(i32), axis=0)
                            gp.indirect_dma_start(agg if l < 3 else agg3, at, tot[:, kk, t, 0:aw[l]], None,
                                                  bounds_check=NP - 1, oob_is_err=False).then_inc(spread[kk], 16)

                if l == 0:
                    gp.wait_ge(zeroed, 16 * (NP * AW // (P * 2025)))
                if l == 3:
                    gp.wait_ge(zeroed3, 16 * (NP * AW3 // (P * 2000)))
                for k in range(RING):
                    wait(gp, stored[k], l * (NBLK // RING) * 16)
                steps(gp, 0, NPAIR + 6, POOL_STEADY, edge_moves)

                to = out if l == 3 else xtab[l + 1]
                xrows = to.rearrange("(b p t) c -> b p t c", p=P, t=BT)

                def node_moves(b, k, turn):
                    if within(b, 0, NBLK):
                        gp.wait_ge(x_in[k], node_slot(l, turn) * 16)
                        gp.wait_ge(a_in[k], node_slot(l, turn) * 16)
                        x0 = xn[:, k, :, F]
                        base = lambda n: (l * NBLK + b) * n if isinstance(b, int) else b * n + l * NBLK * n
                        if l == 2:
                            gp.wait_ge(count_ready, b + 1)
                            wait(gp, y_sum, node_count(l, b - RING))
                            gp.tensor_tensor(gates[:, k, :, 0], x0, inv_count[:, k, 1, :], ALU.mult).then_inc(pool_chain, 1)
                            gp.wait_ge(pool_chain, PC2 + b * 3 + 1)
                            alone(gp, passed["gp"])
                            gp.tensor_tensor(gates[:, k, :, 1], gates[:, k, :, 0], gates[:, k, :, 0], ALU.mult).then_inc(pool_chain, 1)
                            gp.wait_ge(pool_chain, PC2 + b * 3 + 2)
                            alone(gp, passed["gp"])
                            gp.tensor_tensor(gates[:, k, :, 0], gates[:, k, :, 1], an[:, k, :, 0], ALU.mult).then_inc(pool_chain, 1)
                            gp.wait_ge(pool_chain, PC2 + b * 3 + 3)
                            alone(gp, passed["gp"])
                            gp.engine_nop().then_inc(gates_ready, 1)
                        if l == 3:
                            wait(gp, y_sum, node_count(l, b - RING))
                            gp.tensor_tensor(gates[:, k, :, 0], x0, xn[:, k, :, F + 2], ALU.mult)
                            gp.tensor_tensor(gates[:, k, :, 1], xn[:, k, :, F + 1], xn[:, k, :, F + 2], ALU.mult).then_inc(gates_ready, 1)
                        if l == 0:
                            T = trig[:, k]
                            n = [0]

                            def link(ins):
                                ins.then_inc(pool_chain, 1)
                                n[0] += 1
                                gp.wait_ge(pool_chain, b * TRIG_OPS + n[0])
                                alone(gp, passed["gp"])

                            wait(gp, y_sum, node_count(l, b - RING))
                            link(gp.tensor_tensor(T[:, 0, 0, :], an[:, k, :, 0], x0, ALU.mult))
                            link(gp.tensor_copy(T[:, 0, 1, :], T[:, 0, 0, :]))
                            link(gp.tensor_scalar(T[:, 1, 0, :], T[:, 0, 0, :], float(0.5 / np.pi), None, ALU.mult))
                            link(gp.tensor_scalar(T[:, 1, 1, :], T[:, 1, 0, :], 0.25, None, ALU.add))
                            link(gp.tensor_scalar(T[:, 2], T[:, 1], ROUND, None, ALU.add))
                            link(gp.tensor_scalar(T[:, 1], T[:, 2], ROUND, None, ALU.subtract))
                            link(gp.tensor_scalar(T[:, 2], T[:, 1], TWO_PI_HI, None, ALU.mult))
                            link(gp.tensor_tensor(T[:, 3], T[:, 0], T[:, 2], ALU.subtract))
                            link(gp.tensor_scalar(T[:, 2], T[:, 1], TWO_PI_LO, None, ALU.mult))
                            link(gp.tensor_tensor(T[:, 4], T[:, 3], T[:, 2], ALU.subtract))
                            link(gp.tensor_scalar(T[:, 4, 1, :], T[:, 4, 1, :], float(np.pi / 2), None, ALU.add))
                            link(gp.tensor_scalar(T[:, 3], T[:, 4], 3.1415925, -3.1415925, ALU.min, ALU.max))
                            gp.engine_nop().then_inc(trig_ready, 1)
                            gp.wait_ge(sin_ready, b + 1)
                            gp.tensor_tensor(gates[:, k, :, 0], T[:, 5, 0, :], x0, ALU.mult)
                            gp.tensor_tensor(gates[:, k, :, 1], T[:, 5, 1, :], x0, ALU.mult).then_inc(gates_ready, 1)
                    if within(b, 2, NBLK + 2):
                        kk, tt = back(k, turn, 2)
                        b2 = b - 2
                        if not isinstance(b, int):
                            b2 = gp.snap(b2)
                        gp.wait_ge(normed, node_count(l, b - 2))
                        width = F if l == 3 else XW
                        gp.dma_start(xrows[bass.ds(b2, 1)].rearrange("o p t c -> (o p) t c"),
                                     xn[:, kk, :, 0:width]).then_inc(stored[kk], 16)

                steps(gp, 0, NBLK + 2, NODE_STEADY, node_moves)

        @block.tensor
        def _(pe):
            pe.wait_ge(ident_ready, 1)
            pe.wait_ge(viol_ready, 1)
            nc.tensor.matmul(bank[0][0:1, 0:1], viol, ones[0:NPAIR, 0:1], start=True, stop=True).then_inc(viol_summed, 1)
            for t in range(2):
                last = nc.tensor.transpose(bank[1][:, t * NPAIR:(t + 1) * NPAIR], dst0[:, t * P:(t + 1) * P],
                                           ident[0:NPAIR, 0:NPAIR])
            last.then_inc(dcol_turned, 1)
            pe.wait_ge(fields_ready, 1)
            pe.wait_ge(attr_in0, 16)
            rows = attr_rows.rearrange("q (t e c) -> q t e c", t=2, c=EA)
            cols = [f[:, t * P:(t + 1) * P] for f in (src1, idx1, dst1, carry1) for t in range(2)]
            cols += [rows[:, t, :, c] for t in range(2) for c in range(4)]
            for n, c in enumerate(cols):
                o = (n % 4) * NPAIR
                last = nc.tensor.transpose(bank[2 + n // 4][:, o:o + NPAIR], c, ident[0:NPAIR, 0:NPAIR])
            last.then_inc(fields_turned, 1)
            o = STAGE[3]['l2']
            pe.wait_ge(stage_in, 16 * len(LOADS))
            for j in range(4):
                last = nc.tensor.transpose(bank[6][0:96, 96 * j:96 * j + 96], stage[0:96, o + 96 * j:o + 96 * j + 96],
                                           ident[0:96, 0:96])
            last.then_inc(l2_turned, 1)
            pe.wait_ge(l2_copied, 1)
            ot = o + 480
            for j in range(4):
                a, b = (384, 448) if j < 2 else (448, 480)
                at = (0, 64, 128, 160)[j]
                last = nc.tensor.matmul(bank[7][0:MR, at:at + b - a], stage[0:96, ot + MR * j:ot + MR * (j + 1)],
                                        stage[0:96, o + a:o + b], start=True, stop=True)
            last.then_inc(l2_product, 1)
            pe.wait_ge(weights_ready, 1)
            pe.wait_ge(meta_ready, 1)

            for l in range(4):
                L = LAYERS[l]
                G = L["groups"]
                fb = [bank[3], bank[3]] if G == 1 else [bank[3], bank[4]]
                fo = [0, F] if G == 1 else [0, 0]
                tb = [bank[4], bank[7]] if G == 1 else [bank[7], bank[7]]

                def edge_products(q, k, turn):
                    k2 = k % 2
                    if not isinstance(q, int):
                        here = [pe.snap(((NPAIR + 1 - q) * 2 + t) * P) for t in range(2)]
                    else:
                        here = [((NPAIR + 1 - q) * 2 + t) * P for t in range(2)]
                    has_new, has_old = within(q, 0, NPAIR), within(q, 2, NPAIR + 2)
                    if has_new:
                        pe.wait_ge(gathered[k], slot_count(l, k, turn) * 32)
                        pe.wait_ge(ea_in[k], slot_count(l, k, turn) * 16)
                        wait(pe, turned_out, edge_count(l, q - 1))
                        for c, a in ((0, 0), (1, S)):
                            for t in range(2):
                                last = nc.tensor.transpose(bank[0][:, (2 * c + t) * P:(2 * c + t + 1) * P],
                                                           xg[:, k, t, a:a + P], ident[:, :])
                        last.then_inc(turned, 1)
                    if has_old:
                        pe.wait_ge(msg_ready, edge_count(l, q - 2))
                        if l == 0:
                            pe.wait_ge(same_ready, (q - 1) * 2)
                        for t in (1, 0):
                            wait(pe, summed_out[t], edge_count(l, q - 3))
                            alone(pe, passed["pe"])
                            for c in range(4):
                                last = nc.tensor.matmul(bank[5 + t][0:MR, c * P:(c + 1) * P], msg[:, k2, t, c, :],
                                                        same_all[:, bass.ds(here[t], P)], start=True, stop=True)
                            last.then_inc(summed[t], 1)
                    if has_new:
                        pe.wait_ge(turned_out, edge_count(l, q))
                        wait(pe, h_act, edge_count(l, q - 1))
                        nc.tensor.matmul(bank[1][0:L["hid"], 0:256], fc1[l][96:128, :], xT[96:128, k2, 256:512],
                                         start=True, stop=True).then_inc(h_ready, 1)

                    def second_map(t):
                        pe.wait_ge(summed_out[t], edge_count(l, q - 2))
                        if t == 0:
                            pe.wait_ge(carried[0], edge_count(l, q - 2))
                        else:
                            wait(pe, carried[1], edge_count(l, q - 3))
                        if G == 1:
                            wait(pe, tot_out, edge_count(l, q - 3))
                        elif t == 1:
                            wait(pe, tot_out, edge_count(l, q - 3))
                        else:
                            pe.wait_ge(carried_tot, edge_count(l, q - 2))
                        head = 2 + S if G == 1 else 2 * S
                        nc.tensor.matmul(tb[t][:, 0:head], aggT[:, t, 0:P], w2[l][:, t, 0:head], start=True, stop=True)
                        for d in range(3):
                            a, b = head + d * G * V, head + (d + 1) * G * V
                            last = nc.tensor.matmul(tb[t][:, a:b], aggT[:, t, (d + 1) * P:(d + 2) * P],
                                                    w2[l][:, t, a:b], start=True, stop=True)
                        last.then_inc(tot_ready[t], 1)

                    if has_old:
                        second_map(1)
                    if has_new:
                        wait(pe, msg_ready, edge_count(l, q - 1))
                        for t in range(2):
                            for g in range(G):
                                o = fo[t] + g * F
                                nc.tensor.matmul(fb[t][:, o:o + S], xT[0:S, k2, t * P:(t + 1) * P],
                                                 w1s[l][:, g * S:(g + 1) * S], start=True, stop=True)
                                last = nc.tensor.matmul(fb[t][:, o + S:o + F], xT[0:96, k2, (2 + t) * P:(3 + t) * P],
                                                        w1v[l][:, g * 96:(g + 1) * 96], start=True, stop=True)
                        last.then_inc(f_ready, 1)
                        pe.wait_ge(h_act, edge_count(l, q))
                        for t in range(2):
                            last = nc.tensor.matmul(bank[2][:, t * 192:(t + 1) * 192], hT[0:L["hid"], k2, t * P:(t + 1) * P],
                                                    fc2[l][:, :], start=True, stop=True)
                        last.then_inc(w_ready, 1)
                    if has_old:
                        second_map(0)

                steps(pe, 0, NPAIR + 2, EDGE_STEADY, edge_products)

                pe.wait_ge(tot_out, edge_count(l, NPAIR - 1))
                pe.wait_ge(msg_ready, edge_count(l, NPAIR - 1))
                if l == 3:
                    pe.wait_ge(carried_tot, edge_count(l, NPAIR - 1))

                def node_products(b, k, turn):
                    pe.wait_ge(x_in[k], node_slot(l, turn) * 16)
                    base = b * 2 + 2 * l * NBLK
                    for d in range(2):
                        wait(pe, nturned_out, base + (d - 1))
                        for c, a in ((0, 0), (1, S)):
                            for t in range(2):
                                last = nc.tensor.transpose(bank[d][0:96, (2 * c + t) * P:(2 * c + t + 1) * P],
                                                           xn[:, k, 2 * d + t, a:a + 96], ident[:, :])
                        last.then_inc(nturned, 1)
                    for d in range(2):
                        pe.wait_ge(nturned_out, base + (d + 1))
                        if G == 1:
                            wait(pe, y_stt, base + (d - 3))
                        else:
                            wait(pe, y_stt, base + (d - 1))
                        for t in range(2):
                            for g in range(G):
                                ob = bank[2 + 2 * (k % 2) + d] if G == 1 else bank[2 + 2 * d + t]
                                o = t * F if G == 1 else g * F
                                nc.tensor.matmul(ob[:, o:o + S], xT[0:S, d, t * P:(t + 1) * P],
                                                 scs[l][:, g * S:(g + 1) * S], start=True, stop=True)
                                last = nc.tensor.matmul(ob[:, o + S:o + F], xT[0:96, d, (2 + t) * P:(3 + t) * P],
                                                        scv[l][:, g * 96:(g + 1) * 96], start=True, stop=True)
                        last.then_inc(sc_ready, 1)

                steps(pe, 0, NBLK, NODE_STEADY, node_products)
                pe.wait_ge(y_stt, 2 * NBLK * (l + 1))

        @block.scalar
        def _(act):
            act.wait_ge(meta_ready, 1)
            act.wait_ge(weights_ready, 1)
            for l in range(4):
                L = LAYERS[l]
                G = L["groups"]
                fb = [bank[3], bank[3]] if G == 1 else [bank[3], bank[4]]
                tb = [bank[4], bank[7]] if G == 1 else [bank[7], bank[7]]

                def edge_copies(q, k, turn):
                    k2 = k % 2
                    has_new, has_old = within(q, 0, NPAIR), within(q, 2, NPAIR + 2)
                    if has_new:
                        act.wait_ge(turned, edge_count(l, q))
                        wait(act, f_ready, edge_count(l, q - 2))
                        nc.scalar.activation(xT[:, k2, :], bank[0][:, :], ACT.Copy).then_inc(turned_out, 1)
                    if has_old:
                        act.wait_ge(summed[1], edge_count(l, q - 2))
                        wait(act, tot_ready[1], edge_count(l, q - 3))
                        nc.scalar.activation(aggT[:, 1, :], bank[6][0:MR, :], ACT.Copy).then_inc(summed_out[1], 1)
                    if has_new:
                        act.wait_ge(h_ready, edge_count(l, q))
                        wait(act, w_ready, edge_count(l, q - 2))
                        nc.scalar.activation(hT[0:L["hid"], k2, :], bank[1][0:L["hid"], 0:256],
                                             ACT.Silu if L["silu"] else ACT.Relu, scale=L["hs"]).then_inc(h_act, 1)

                    def totals(t):
                        kk, tt = back(k, turn, 2)
                        act.wait_ge(tot_ready[t], edge_count(l, q - 2))
                        nc.scalar.activation(w2[l][0:1, 1 - t, :], tb[t][0:1, 0:aw[l]], ACT.Copy).then_inc(carried[1 - t], 1)
                        if t == 1 and (l or within(q, 6, NPAIR + 6)):
                            k6, t6 = back(k, turn, 6)
                            wait(act, spread[k6], slot_count(l, k6, t6) * 32)
                        if G == 1:
                            nc.scalar.activation(tot[:, kk, t, 0:2 + S], tb[t][:, 0:2 + S], ACT.Copy)
                            last = nc.scalar.activation(tot[:, kk, t, 2 + S:AW].rearrange("p (v d) -> p v d", d=3),
                                                        tb[t][:, 2 + S:AW].rearrange("p (d v) -> p v d", d=3), ACT.Copy)
                        else:
                            to = tot[:, kk, t, :].rearrange("p (g c) -> p g c", g=2)
                            nc.scalar.activation(to[:, :, 0:S], tb[t][:, 0:2 * S].rearrange("p (g c) -> p g c", g=2), ACT.Copy)
                            of = tb[t][:, 2 * S:AW3].rearrange("p (d g v) -> p g v d", d=3, g=2)
                            for g in range(2):
                                last = nc.scalar.activation(to[:, g, S:F].rearrange("p (v d) -> p v d", d=3),
                                                            of[:, g], ACT.Copy)
                        last.then_inc(tot_out if t == 0 else carried_tot, 1)

                    if has_old:
                        totals(1)
                    if has_new and G == 2:
                        act.wait_ge(f_ready, edge_count(l, q))
                        wait(act, msg_ready, edge_count(l, q - 2))
                        for t in range(2):
                            last = nc.scalar.activation(fsum[:, k2, t, :], fb[t][:, 0:F], ACT.Copy,
                                                        scale=xg[:, k, t, F:F + 1])
                        last.then_inc(fa_out, 1)
                    if has_old:
                        totals(0)

                steps(act, 0, NPAIR + 2, EDGE_STEADY, edge_copies)

                def node_copies(b, k, turn):
                    if within(b, 0, NBLK):
                        base = b * 2 + 2 * l * NBLK
                        for d in range(2):
                            act.wait_ge(nturned, base + (d + 1))
                            wait(act, sc_ready, base + (d - 1))
                            nc.scalar.activation(xT[0:96, d, :], bank[d][0:96, :], ACT.Copy).then_inc(nturned_out, 1)
                        if l == 0:
                            act.wait_ge(trig_ready, b + 1)
                            nc.scalar.activation(trig[:, k, 5], trig[:, k, 3], ACT.Sin).then_inc(sin_ready, 1)
                    if within(b, 1, NBLK + 1):
                        kk, tt = back(k, turn, 1)
                        act.wait_ge(mv_ready, node_count(l, b - 1))
                        nc.scalar.activation(std[:, kk, :], mv[:, kk, :, 1], ACT.Sqrt, bias=eps[:, :]).then_inc(std_ready, 1)
                        act.wait_ge(shift_ready, node_count(l, b - 1))
                        for t in range(BT):
                            last = nc.scalar.activation(xn[:, kk, t, 0:F], yn[:, kk, t, :], ACT.Identity,
                                                        bias=shift[:, kk, t:t + 1], scale=rstd[:, kk, t:t + 1])
                        last.then_inc(normed, 1)

                steps(act, 0, NBLK + 1, NODE_STEADY, node_copies)

        @block.vector
        def _(dve):
            count = [0]

            def link(ins):
                count[0] += 1
                ins.then_inc(chain, 1)
                dve.wait_ge(chain, count[0])

            nc.vector.memset(prev0, -1)
            nc.vector.memset(ones[:, :], 1.0)
            nc.vector.memset(eps[:, :], EPS)
            link(nc.vector.memset(zeros[:, :], 0.0))
            dve.engine_nop().then_inc(filled, 1)
            dve.wait_ge(given_in, 48)
            nc.vector.tensor_copy(dst0, pairs0.rearrange("q (e c) -> q e c", c=2)[:, :, 1])
            link(nc.vector.tensor_copy(prv0, prev0.rearrange("q (e c) -> q e c", c=2)[:, :, 1]))
            link(nc.vector.tensor_tensor(less0, dst0, prv0, ALU.is_lt))
            nc.vector.tensor_reduce(viol, less0, AX.X, ALU.max).then_inc(viol_ready, 1)
            dve.wait_ge(viol_summed, 1)
            nc.vector.tensor_scalar(flag, bank[0][0:1, 0:1], 0.5, None, ALU.is_gt).then_inc(flag_ready, 1)
            dve.wait_ge(dcol_turned, 1)
            link(nc.vector.tensor_copy(dcol0.rearrange("p q t -> p t q"),
                                       bank[1][:, 0:2 * NPAIR].rearrange("p (t q) -> p t q", t=2)))
            dve.wait_ge(flag_ready, 1)
            unsorted = dve.value_load(flag, min_val=0, max_val=1)
            with dve.If(unsorted > 0):
                dve.wait_ge(iota_ready, 2)
                edge, rank, lesser, equal, start = (sort_s[:, c:c + 1] for c in (1, 2, 3, 4, 5))
                nc.vector.tensor_copy(sort_iota, sort_a.bitcast(i32)).then_inc(sort_chain, 1)
                nc.vector.tensor_copy(edge, sort_s[:, 0:1].bitcast(i32)).then_inc(sort_chain, 1)
                dve.wait_ge(sort_chain, 2)
                dve.wait_ge(bcast_in, 16)
                dall = dcol0.rearrange("p q t -> p (q t)")
                CH = EP // SORT_COLS
                per = 4 + CH * 7

                with dve.Fori(0, NT) as t:
                    n = [0]

                    def then(ins, at):
                        ins.then_inc(sort_chain, 1)
                        dve.wait_ge(sort_chain, at)
                        alone(dve, passed["dve"])

                    b0 = t * per + 2
                    then(nc.vector.tensor_copy(sort_s[:, 6:7], dall[:, bass.ds(t, 1)]), b0 + 1)
                    then(nc.vector.memset(rank, 0.0), b0 + 2)
                    then(nc.vector.tensor_copy(start, edge), b0 + 3)
                    with dve.Fori(0, CH) as c:
                        b1 = t * per + c * 7 + 5
                        cols = same_all[:, bass.ds(c * SORT_COLS, SORT_COLS)]
                        then(nc.vector.tensor_scalar(sort_a, cols, sort_s[:, 6:7], None, ALU.is_lt), b1 + 1)
                        then(nc.vector.tensor_reduce(lesser, sort_a, AX.X, ALU.add), b1 + 2)
                        then(nc.vector.tensor_scalar(sort_b, cols, sort_s[:, 6:7], None, ALU.is_equal), b1 + 3)
                        then(nc.vector.scalar_tensor_tensor(out=sort_a, in0=sort_iota, scalar=start, in1=sort_b,
                                                            op0=ALU.is_lt, op1=ALU.mult), b1 + 4)
                        then(nc.vector.tensor_reduce(equal, sort_a, AX.X, ALU.add), b1 + 5)
                        then(nc.vector.scalar_tensor_tensor(out=rank, in0=lesser, scalar=equal, in1=rank,
                                                            op0=ALU.add, op1=ALU.add), b1 + 6)
                        then(nc.vector.tensor_scalar(start, start, float(SORT_COLS), None, ALU.subtract), b1 + 7)
                    dve.wait_ge(ranks_free, t + 1)
                    nc.vector.tensor_copy(sort_s[:, 8:9].bitcast(i32), rank).then_inc(pos_ready, 1)
                    then(nc.vector.tensor_scalar(edge, edge, float(P), None, ALU.add), t * per + (per + 2))

            dve.wait_ge(records_ready, 1)
            nc.vector.memset(stage, 0.0)
            nc.vector.memset(prev1, -1)
            nc.vector.memset(next1, -1)
            for l in range(4):
                nc.vector.memset(fc1[l][96:128, :], 0.0)
            nc.vector.memset(carry1, 0.0)
            nc.vector.memset(xg[:, :, :, :], 0.0)
            nc.vector.memset(msg[:, :, :, :, MR - 1:MR], 1.0)
            link(nc.vector.memset(meta_all[:, :, 14:16], 0.0))
            dve.engine_nop().then_inc(stage_zero, 1)
            dve.wait_ge(rows_in, 64)
            two = lambda ap: ap.rearrange("q (e c) -> q e c", c=2)
            nc.vector.tensor_copy(dst1, two(pairs1)[:, :, 1])
            nc.vector.tensor_copy(src1, two(pairs1)[:, :, 0])
            nc.vector.tensor_copy(nxt1, next1[:, 1:2])
            link(nc.vector.tensor_copy(prv1, two(prev1)[:, :, 1]))
            assert count[0] == CHAIN_DST
            link(nc.vector.tensor_tensor(same1, dst1, prv1, ALU.is_equal))
            nc.vector.scalar_tensor_tensor(out=idx1, in0=same1, scalar=FAR, in1=dst1, op0=ALU.mult, op1=ALU.add)
            nc.vector.tensor_tensor(carry1[:, 127:128], dst1[:, 127:128], dst1[:, 128:129], ALU.is_equal)
            link(nc.vector.tensor_tensor(carry1[:, 255:256], dst1[:, 255:256], nxt1, ALU.is_equal))
            dve.engine_nop().then_inc(fields_ready, 1)
            dve.wait_ge(fields_turned, 1)
            four = lambda b: b[:, 0:4 * NPAIR].rearrange("p (f q) -> p f q", f=4)
            by_field = lambda ap: ap.rearrange("p q f -> p f q")
            nc.vector.tensor_copy(by_field(meta_all[:, :, 0:4].bitcast(i32)), four(bank[2]))
            nc.vector.tensor_copy(by_field(dst_col[:, :, :]), four(bank[3])[:, 0:2])
            nc.vector.tensor_copy(by_field(meta_all[:, :, 4:6]), four(bank[3])[:, 2:4])
            nc.vector.tensor_copy(by_field(meta_all[:, :, 6:10]), four(bank[4]))
            link(nc.vector.tensor_copy(by_field(meta_all[:, :, 10:14]), four(bank[5])))
            dve.engine_nop().then_inc(meta_ready, 1)
            dve.wait_ge(stage_in, 16 * len(LOADS))
            scaled = lambda to, of, c: nc.vector.tensor_scalar(to, of, float(c), None, ALU.mult)
            for l, L in enumerate(LAYERS):
                st, hid, G = STAGE[l], L["hid"], L["groups"]
                scaled(fc2[l][:, 0:160], stage[0:hid, st['fc2']:st['fc2'] + 160], L["w"])
                scaled(fc2[l][:, 160:192], stage[0:hid, st['fc2'] + 160:st['fc2'] + 192], L["w"] * R3)
                scaled(w1s[l][:, :], stage[0:S, st['w1s']:st['w1s'] + G * S], L["fs"])
                scaled(w1v[l][:, :], stage[0:96, st['w1v']:st['w1v'] + G * 96], L["fv"])
                scaled(scs[l][:, :], stage[0:S, st['scs']:st['scs'] + G * S], L["sc"])
                for g in range(G):
                    of = stage[0:96, st['scv'] + g * 96:st['scv'] + (g + 1) * 96]
                    scaled(scv[l][:, g * 96:(g + 1) * 96].rearrange("p (v d) -> p v d", d=3),
                           of.rearrange("p (d v) -> p v d", d=3), L["scv"])
                if l < 3:
                    for t in range(2):
                        o = st['w2']
                        scaled(w2[l][:, t, 0:1], stage[0:MR, o:o + 1], L["extra"])
                        scaled(w2[l][:, t, 1:2], stage[0:MR, o + 1:o + 2], 1.0)
                        scaled(w2[l][:, t, 2:AW], stage[0:MR, o + 2:o + AW], L["conv"])
            dve.wait_ge(l2_turned, 1)
            ot = STAGE[3]['l2'] + 480
            nc.vector.tensor_copy(stage[0:96, ot:ot + 4 * MR].rearrange("p (j c) -> p j c", j=4)[:, :, 1:97],
                                  bank[6][0:96, 0:384].rearrange("p (j c) -> p j c", j=4)).then_inc(l2_copied, 1)
            dve.wait_ge(l2_product, 1)
            c = LAYERS[3]["conv"]
            for t in range(2):
                scaled(w2[3][:, t, 0:128], bank[7][0:MR, 0:128], c)
                for d in range(3):
                    last = scaled(w2[3][:, t, 128 + 64 * d:192 + 64 * d], bank[7][0:MR, 128:192], c)
            link(last)
            dve.engine_nop().then_inc(weights_ready, 1)
            dve.wait_ge(dst_in, 64)
            dflat = dst_col[:, :, :].rearrange("p q t -> p (q t)")
            with dve.Fori(0, NPAIR) as i:
                for t in (1, 0):
                    tile = (NPAIR - 1 - i) * 2 + t
                    cols = same_all[:, bass.ds(tile * P, P)]
                    nc.vector.tensor_scalar(cols, cols, dflat[:, bass.ds(tile, 1)], None, ALU.is_equal).then_inc(same_ready, 1)

            for l in range(4):
                L = LAYERS[l]
                G = L["groups"]

                def edge_vectors(q, k, turn):
                    k2 = k % 2
                    if within(q, 2, NPAIR + 2):
                        dve.wait_ge(summed[0], edge_count(l, q - 2))
                        wait(dve, tot_ready[0], edge_count(l, q - 3))
                        nc.vector.tensor_copy(aggT[:, 0, :], bank[5][0:MR, :]).then_inc(summed_out[0], 1)
                    if not within(q, 0, NPAIR):
                        return
                    dve.wait_ge(meta_in[k], slot_count(l, k, turn) * 16)
                    sh = meta[:, k, 6:14].rearrange("p (t c) -> p t c", t=2)
                    if G == 1:
                        dve.wait_ge(gathered[k], slot_count(l, k, turn) * 32)
                        wait(dve, msg_ready, edge_count(l, q - 1))
                        nc.vector.tensor_tensor(yv[:, k2], sh, xg[:, k, :, F:F + 1].to_broadcast([P, 2, 4]), ALU.mult)\
                            .then_inc(y_ready, 1)
                        y = yv[:, k2]
                        dve.wait_ge(y_ready, edge_count(l, q))
                    else:
                        y = sh
                        wait(dve, msg_ready, edge_count(l, q - 1))
                    dve.wait_ge(w_ready, edge_count(l, q))
                    wt = bank[2][:, 0:384].rearrange("p (t c) -> p t c", t=2)
                    nc.vector.tensor_tensor(wy[:, k2, :, 0, :], wt[:, :, 0:96], y[:, :, 0:1].to_broadcast([P, 2, 96]), ALU.mult)
                    nc.vector.tensor_tensor(wy[:, k2, :, 1:4, :],
                                            wt[:, :, None, 96:192].to_broadcast([P, 2, 3, 96]),
                                            y[:, :, 1:4, None].to_broadcast([P, 2, 3, 96]), ALU.mult).then_inc(wy_ready, 1)
                    if G == 1:
                        dve.wait_ge(f_ready, edge_count(l, q))
                        f = bank[3][:, 0:2 * F].rearrange("p (t c) -> p t c", t=2)
                    else:
                        dve.wait_ge(fa_out, q + 1)
                        for t in range(2):
                            last = nc.vector.scalar_tensor_tensor(out=fsum[:, k2, t, :], in0=bank[3 + t][:, F:2 * F],
                                                                  scalar=xg[:, k, t, F + 1:F + 2], in1=fsum[:, k2, t, :],
                                                                  op0=ALU.mult, op1=ALU.add)
                        last.then_inc(f_summed, 1)
                        dve.wait_ge(f_summed, q + 1)
                        f = fsum[:, k2]
                    dve.wait_ge(wy_ready, edge_count(l, q))
                    fv = f[:, :, S:F].rearrange("p t (d v) -> p t d v", d=3)
                    nc.vector.tensor_tensor(dprod[:, :, :, :], wy[:, k2, :, 1:4, S:96], fv, ALU.mult).then_inc(dprod_ready, 1)
                    nc.vector.tensor_tensor(msg[:, k2, :, :, 1:1 + S], wy[:, k2, :, :, 0:S],
                                            f[:, :, None, 0:S].to_broadcast([P, 2, 4, S]), ALU.mult)
                    nc.vector.tensor_tensor(msg[:, k2, :, 1:4, 1 + S:97],
                                            wy[:, k2, :, 0:1, S:96].to_broadcast([P, 2, 3, V]), fv, ALU.mult)
                    nc.vector.tensor_copy(msg[:, k2, :, :, 0], meta[:, k, 4:6, None].to_broadcast([P, 2, 4]))
                    dve.wait_ge(dprod_ready, edge_count(l, q))
                    nc.vector.tensor_reduce(msg[:, k2, :, 0, 1 + S:97], dprod[:, :, :, :].rearrange("p t d v -> p t v d"),
                                            AX.X, ALU.add).then_inc(msg_ready, 1)

                steps(dve, 0, NPAIR + 2, EDGE_STEADY, edge_vectors)

                abuf = an if l < 3 else an3

                def node_vectors(b, k, turn):
                    k2 = k % 2
                    base = b * 2 + 2 * l * NBLK

                    def finish():
                        kk, tt = back(k, turn, 1)
                        dve.wait_ge(std_ready, node_count(l, b - 1))
                        nc.vector.reciprocal(rstd[:, kk, :], std[:, kk, :]).then_inc(rstd_ready, 1)
                        dve.wait_ge(rstd_ready, node_count(l, b - 1))
                        nc.vector.scalar_tensor_tensor(out=shift[:, kk, :], in0=mv[:, kk, :, 0], scalar=-1.0,
                                                       in1=rstd[:, kk, :], op0=ALU.mult, op1=ALU.mult).then_inc(shift_ready, 1)

                    if not within(b, 0, NBLK):
                        return finish()
                    dve.wait_ge(x_in[k], node_slot(l, turn) * 16)
                    if l == 2:
                        dve.wait_ge(a_in[k], node_slot(l, turn) * 16)
                        wait(dve, gates_ready, b + (NBLK + 1 - RING))
                        nc.vector.tensor_scalar(inv_count[:, k, 0, :], an[:, k, :, 1], 1.0, None, ALU.max).then_inc(count_max, 1)
                        dve.wait_ge(count_max, b + 1)
                        nc.vector.reciprocal(inv_count[:, k, 1, :], inv_count[:, k, 0, :]).then_inc(count_ready, 1)
                    if l == 0:
                        dve.wait_ge(gates_ready, b + 1)
                    wait(dve, normed, node_count(l, b - RING))
                    for d in range(2):
                        dve.wait_ge(sc_ready, base + (d + 1))
                        for t in range(2):
                            j = 2 * d + t
                            g = gates[:, k, j, 1:2] if l == 0 else xn[:, k, j, F:F + 1]
                            ob = bank[2 + 2 * (k % 2) + d][:, t * F:(t + 1) * F] if G == 1 else bank[2 + j][:, 0:F]
                            last = nc.vector.scalar_tensor_tensor(out=yn[:, k, j, :], in0=ob, scalar=g,
                                                                  in1=xn[:, k, j, 0:F], op0=ALU.mult, op1=ALU.add)
                        if G == 1:
                            last.then_inc(y_stt, 1)
                        else:
                            last.then_inc(y_half, 1)
                            dve.wait_ge(y_half, b * 2 + (d + 1))
                            for t in range(2):
                                j = 2 * d + t
                                last = nc.vector.scalar_tensor_tensor(out=yn[:, k, j, :], in0=bank[2 + j][:, F:2 * F],
                                                                      scalar=xn[:, k, j, F + 1:F + 2], in1=yn[:, k, j, :],
                                                                      op0=ALU.mult, op1=ALU.add)
                            last.then_inc(y_stt, 1)
                        if d == 0 and within(b, 1, NBLK):
                            finish()
                    dve.wait_ge(a_in[k], node_slot(l, turn) * 16)
                    if l == 2:
                        dve.wait_ge(gates_ready, b + (NBLK + 1))
                    if l == 3:
                        dve.wait_ge(gates_ready, b + (2 * NBLK + 1))
                    dve.wait_ge(y_stt, base + 2)
                    for g in range(G):
                        for j in range(BT):
                            gate = xn[:, k, j, F:F + 1] if l == 1 else gates[:, k, j, g:g + 1]
                            a = abuf[:, k, j, 2:AW] if G == 1 else abuf[:, k, j, g * F:(g + 1) * F]
                            last = nc.vector.scalar_tensor_tensor(out=yn[:, k, j, :], in0=a, scalar=gate, in1=yn[:, k, j, :],
                                                                  op0=ALU.mult, op1=ALU.add)
                        if g < G - 1:
                            last.then_inc(y_part, 1)
                            dve.wait_ge(y_part, b + 1)
                    last.then_inc(y_sum, 1)
                    dve.wait_ge(y_sum, node_count(l, b))
                    for j in range(BT):
                        last = nc.vector.bn_stats(stats[:, k2, j, :], yn[:, k, j, :])
                    last.then_inc(stats_ready, 1)
                    dve.wait_ge(stats_ready, node_count(l, b))
                    alone(dve, passed["dve"])
                    for j in range(BT):
                        last = nc.vector.bn_aggr(mv[:, k, j, :], stats[:, k2, j, :])
                    last.then_inc(mv_ready, 1)

                steps(dve, 0, NBLK + 1, NODE_STEADY, node_vectors)


_INTS = ["pairs"]


def kernel(**inputs):
    import concourse.bacc as bacc
    from concourse.bass_utils import run_bass_kernel_spmd

    a = {n: np.asarray(v) for n, v in inputs.items()}
    rows = lambda n, fill=0: np.full((n, 1), fill)
    nodes = np.concatenate([a["x"], a["node_vec1"], a["node_vec1_n2"], a["node_vec1_n3"],
                            np.zeros((N_NODES, 1), np.float32)], axis=1)
    nodes = np.concatenate([nodes, np.zeros((NP - N_NODES, XW), np.float32)], axis=0)
    pad = EP - N_EDGES
    pairs = np.stack([np.concatenate([a["src"], np.zeros(pad, np.int32)]),
                      np.concatenate([a["dst"], np.full(pad, N_NODES, np.int32)])], axis=1)
    eattr = np.concatenate([a["edge_attr_4"], a["edge_attr_8"], a["edge_attr_10"], a["edge_attr_16"]], axis=1)
    eattr = np.concatenate([eattr, np.zeros((pad, EA), np.float32)], axis=0)
    arrays = {"nodes": nodes, "pairs": pairs, "eattr": eattr, **{n: a[n] for n in WEIGHTS}}
    arrays = {n: np.ascontiguousarray(v) for n, v in arrays.items()}

    nc = bacc.Bacc("TRN2", target_bir_lowering=False, num_devices=1)
    given = {n: nc.dram_tensor(n, v.shape, mybir.dt.from_np(v.dtype), kind="ExternalInput").ap()
             for n, v in arrays.items()}
    out = nc.dram_tensor("out", (NP, F), mybir.dt.float32, kind="ExternalOutput").ap()
    build(nc, given["nodes"], given["pairs"], given["eattr"], given, out)
    got = run_bass_kernel_spmd(nc, [arrays], core_ids=[0])
    return got.results[0]["out"][:N_NODES]
```

```python
import numpy as np
import concourse.bass as bass
from concourse import mybir
from contextlib import ExitStack

N_NODES, N_EDGES = 50000, 25000
S, V = 64, 32
F = S + 3 * V
XW = F + 4
P = 128
BT = 4
NBLK = 100
NP = NBLK * BT * P
NPAIR = 98
NT = 2 * NPAIR
EP = NT * P
EA = 38
RING = 4
NRING = 6
AW = 2 + F
AW3 = 2 * F
XC = 192
MR = 2 + S + V
FAR = 262144.0
R3 = float(1.0 / np.sqrt(3.0))
C_S, C_X = float(np.sin(np.pi / 8.0)), float(np.cos(np.pi / 8.0))
EPS = 1e-5
SORT_COLS = 784
TWO_PI_HI = 6.28125
TWO_PI_LO = float(2 * np.pi - 6.28125)
GUESS = float(0x5f3759df)
ROUND = 12582912.0

r = lambda n: float(1.0 / np.sqrt(float(n)))
LAYERS = [
    dict(rad=8, at=4, hid=64, silu=True, hs=r(8), w=r(64), fs=r(64), fv=r(32), sc=r(64), scv=r(32),
         conv=r(10) * r(96), extra=0.1 * r(10) * r(96), groups=1),
    dict(rad=10, at=12, hid=100, silu=False, hs=r(10), w=float(np.sqrt(2.0)) * r(100), fs=r(64), fv=r(32),
         sc=r(64), scv=r(32), conv=0.5 * 0.25 * r(96), extra=1.0, groups=1),
    dict(rad=16, at=22, hid=64, silu=True, hs=r(16), w=r(64), fs=r(64), fv=r(32), sc=r(64), scv=r(32),
         conv=r(96), extra=r(96), groups=1),
    dict(rad=10, at=12, hid=100, silu=True, hs=1.0, w=1.0, fs=1.0, fv=1.0, sc=C_S, scv=C_S,
         conv=C_X * 0.25, extra=1.0, groups=2),
]

WEIGHTS = ['L0_gnn_W_sc_s', 'L0_gnn_W_sc_v', 'L0_gnn_W1_s', 'L0_gnn_W1_v', 'L0_gnn_W2_s', 'L0_gnn_W2_v',
           'L0_gnn_W3', 'L0_gnn_fcW1', 'L0_gnn_fcW2', 'L1_gnn_W_si0', 'L1_gnn_W_si1', 'L1_gnn_W_l1_0',
           'L1_gnn_W_l1_1', 'L1_gnn_W_l2_00', 'L1_gnn_W_l2_10', 'L1_gnn_W_l2_01', 'L1_gnn_W_l2_11',
           'L1_gnn_W_fc1', 'L1_gnn_W_fc2', 'L2_gnn_Wfc1', 'L2_gnn_Wfc2', 'L2_gnn_Wsc0', 'L2_gnn_Wsc1',
           'L2_gnn_Wl1_0', 'L2_gnn_Wl1_1', 'L2_gnn_Wl2_s', 'L2_gnn_Wl2_v', 'L2_gnn_Wa', 'L3_gnn_Ws_sc_a',
           'L3_gnn_Wv_sc_a', 'L3_gnn_Ws_sc_c', 'L3_gnn_Wv_sc_c', 'L3_gnn_Ws_l1_a', 'L3_gnn_Wv_l1_a',
           'L3_gnn_Ws_l1_c', 'L3_gnn_Wv_l1_c', 'L3_gnn_W_fc1', 'L3_gnn_W_fc2', 'L3_gnn_Ws_l2_a',
           'L3_gnn_Wv_l2_a', 'L3_gnn_Ws_l2_c', 'L3_gnn_Wv_l2_c', 'L3_gnn_Ws_l3', 'L3_gnn_Wv_l3']


def back(k, turn, lag, ring=RING):
    return (k - lag) % ring, turn + (k - lag) // ring


def steps(eng, first, last, steady, body, ring=RING):
    lo, hi = steady
    for q in range(first, lo):
        body(q, q % ring, q // ring)
    with eng.Fori(0, (hi - lo) // ring) as i:
        for k in range(ring):
            body(i * ring + (lo + k), k, i + lo // ring)
    for q in range(hi, last):
        body(q, q % ring, q // ring)


def within(q, lo, hi):
    return lo <= q < hi if isinstance(q, int) else True


def wait(eng, sem, value):
    if isinstance(value, int) and value <= 0:
        return
    eng.wait_ge(sem, value)


def alone(eng, passed):
    eng.sem_inc(passed, 1)


def build(nc, nodes, pairs, eattr, w, out):
    f32, i32 = mybir.dt.float32, mybir.dt.int32
    ALU, ACT, AX = mybir.AluOpType, mybir.ActivationFunctionType, mybir.AxisListType
    ctx = ExitStack()
    with ctx:
        def sb(name, shape, dt=f32):
            return ctx.enter_context(nc.sbuf_tensor(name, shape, dt))

        def sem(name):
            return ctx.enter_context(nc.semaphore(name))

        def sems(name, n):
            return [sem(f"{name}{i}") for i in range(n)]

        xtab = [nodes] + [nc.dram_tensor(f"x_after_{l}", (NP, XW), f32, kind="Internal").ap() for l in range(3)]
        agg = nc.dram_tensor("aggregates", (NP, AW), f32, kind="Internal").ap()
        agg3 = nc.dram_tensor("aggregates_3", (NP, AW3), f32, kind="Internal").ap()
        rec_pairs = nc.dram_tensor("sorted_pairs", (EP, 2), i32, kind="Internal").ap()
        rec_attr = nc.dram_tensor("sorted_attr", (EP, EA), f32, kind="Internal").ap()
        dst_row = nc.dram_tensor("sorted_dst", (1, EP), f32, kind="Internal").ap()
        dst_row0 = nc.dram_tensor("given_dst", (1, EP), f32, kind="Internal").ap()

        same_all = sb("same_all", [P, EP])
        meta_all = sb("meta_all", [P, NPAIR, 16])
        dst_col = sb("dst_col", [P, NPAIR, 2])
        ident = sb("ident", [P, P])
        ones = sb("ones", [P, 1])
        half_pi = sb("half_pi", [P, 1])
        eps = sb("eps", [P, 1])
        zeros = sb("zeros", [P, 2025])
        fc1 = [sb(f"fc1_{l}", [P, L["hid"]]) for l, L in enumerate(LAYERS)]
        fc2 = [sb(f"fc2_{l}", [L["hid"], 192]) for l, L in enumerate(LAYERS)]
        w1s = [sb(f"w1s_{l}", [S, L["groups"] * S]) for l, L in enumerate(LAYERS)]
        w1v = [sb(f"w1v_{l}", [96, L["groups"] * 96]) for l, L in enumerate(LAYERS)]
        sc_head = [sb(f"sc_head_{l}", [P, F]) for l in range(3)]
        sc_tail = [sb(f"sc_tail_{l}", [P, 96]) for l in range(3)]
        scs3 = sb("scs_3", [S, 2 * S])
        scv3 = sb("scv_3", [96, 2 * 96])
        aw = [AW, AW, AW, AW3]
        w2 = [sb(f"w2_{l}", [MR, 2, aw[l]]) for l in range(4)]

        meta = sb("meta", [P, RING, 16])
        sidx = sb("sidx", [P, RING, 2])
        xg = sb("xg", [P, RING, 2, XC])
        xT = sb("xT", [P, 2, 512])
        yv = sb("yv", [P, 2, 2, 4])
        msg = sb("msg", [P, 2, 2, 4, MR])
        dprod = sb("dprod", [P, 2, 3, 32])

        arena = sb("arena", [P, NRING * BT * (XW + AW + XW)])
        o1, o2, o3, o4 = 512, 512 + 4 * 384, 512 + 4 * 384 + 4 * F, 1536 + 4 * 384 + 4 * F
        hT = arena[0:100, 0:o1].rearrange("p (b c) -> p b c", b=2)
        wy = arena[:, o1:o2].rearrange("p (b t h c) -> p b t h c", b=2, t=2, h=4)
        fsum = arena[:, o2:o3].rearrange("p (b t c) -> p b t c", b=2, t=2)
        aggT = arena[0:MR, o3:o4].rearrange("p (t c) -> p t c", t=2)
        tot = arena[:, o4:o4 + RING * 2 * AW3].rearrange("p (r t c) -> p r t c", r=RING, t=2)
        n1 = NRING * BT * XW
        n2 = n1 + NRING * BT * AW
        xn = arena[:, 0:n1].rearrange("p (r t c) -> p r t c", r=NRING, t=BT)
        an = arena[:, n1:n2].rearrange("p (r t c) -> p r t c", r=NRING, t=BT)
        yn = arena[:, n2:n2 + n1].rearrange("p (r t c) -> p r t c", r=NRING, t=BT)
        an3 = same_all[:, 0:NRING * BT * AW3].rearrange("p (r t c) -> p r t c", r=NRING, t=BT)
        stats = sb("stats", [P, 2, BT, 6])
        mv = sb("mv", [P, NRING, BT, 2])
        std = sb("std", [P, NRING, BT])
        var = sb("var", [P, 2, BT])
        newton = sb("newton", [P, 2, 3, BT])
        rstd = sb("rstd", [P, NRING, BT])
        shift = sb("shift", [P, NRING, BT])
        gates = sb("gates", [P, NRING, BT, 2])
        trig = sb("trig", [P, NRING, 6, BT])
        waves = sb("waves", [P, NRING, 2, BT])
        inv_count = sb("inv_count", [P, NRING, 2, BT])

        def part(a, n, rows=NPAIR):
            return arena[0:rows, a:a + n]

        pairs0 = part(0, 512).bitcast(i32)
        prev0 = part(512, 512).bitcast(i32)
        dst0 = part(1024, 256)
        prv0 = part(1280, 256)
        less0 = part(1536, 256)
        viol = part(1792, 1)
        dcol0 = arena[:, 1800:1800 + 2 * NPAIR].rearrange("p (q t) -> p q t", t=2)
        flag = part(1996, 1, 1).bitcast(i32)
        pairs1 = part(2000, 512).bitcast(i32)
        prev1 = part(2512, 512).bitcast(i32)
        next1 = part(3024, 2).bitcast(i32)
        dst1 = part(3028, 256)
        src1 = part(3284, 256)
        prv1 = part(3540, 256)
        nxt1 = part(3796, 1)
        same1 = part(3800, 256)
        idx1 = part(4056, 256)
        carry1 = part(4312, 256)
        sort_iota = arena[:, 4600:4600 + SORT_COLS]
        sort_a = arena[:, 5400:5400 + SORT_COLS]
        sort_b = arena[:, 6200:6200 + SORT_COLS]
        sort_s = arena[:, 7000:7016]
        sort_pair = arena[:, 7020:7022].bitcast(i32)
        sort_attr = arena[:, 7024:7024 + EA]
        attr_rows = same_all[0:NPAIR, 4096:4096 + 256 * EA]
        stage = arena[:, 7100:7100 + 4096]

        bank = [ctx.enter_context(nc.psum_tensor(f"bank{i}", [P, 512], f32)) for i in range(8)]

        passed = {e: sem(f"passed_{e}") for e in ("sp", "gp", "pe", "dve", "act")}
        filled = sem("filled")
        given_in, given_seen = sem("given_in"), sem("given_seen")
        viol_ready, viol_summed, flag_ready = sem("viol_ready"), sem("viol_summed"), sem("flag_ready")
        dcol_turned = sem("dcol_turned")
        copied, sort_dma, pos_ready, sort_io, sort_chain = (sem("copied"), sem("sort_dma"), sem("pos_ready"),
                                                            sem("sort_io"), sem("sort_chain"))
        ranks_free = sem("ranks_free")
        bcast_in, scattered, iota_ready = sem("bcast_in"), sem("scattered"), sem("iota_ready")
        records_ready = sem("records_ready")
        rows_blank = sem("rows_blank")
        stage_zero, rows_in, attr_in0, stage_in = sem("stage_zero"), sem("rows_in"), sem("attr_in0"), sem("stage_in")
        ident_ready, ident_a = sem("ident_ready"), sem("ident_a")
        chain = sem("chain")
        fields_ready, fields_turned = sem("fields_ready"), sem("fields_turned")
        l2_turned, l2_copied, l2_product = sem("l2_turned"), sem("l2_copied"), sem("l2_product")
        dst_out, dst_in, weights_ready, same_ready = sem("dst_out"), sem("dst_in"), sem("weights_ready"), sem("same_ready")
        dst_in_first, records_seen = sem("dst_in_first"), sem("records_seen")
        meta_ready = sem("meta_ready")
        CHAIN_DST = 8
        zeroed, zeroed3 = sem("zeroed"), sem("zeroed3")

        meta_in, ea_in, sidx_in = sems("meta_in", RING), sems("ea_in", RING), sems("sidx_in", RING)
        gathered, spread = sems("gathered", RING), sems("spread", RING)
        turned, turned_out = sem("turned"), sem("turned_out")
        h_ready, h_act, f_ready, w_ready = sem("h_ready"), sem("h_act"), sem("f_ready"), sem("w_ready")
        y_ready, wy_ready, dprod_ready, msg_ready = sem("y_ready"), sem("wy_ready"), sem("dprod_ready"), sem("msg_ready")
        fa_out, f_summed = sem("fa_out"), sem("f_summed")
        carried_tot = sem("carried_tot")
        summed, summed_out = sems("summed", 2), sems("summed_out", 2)
        tot_ready, carried, tot_out = sems("tot_ready", 2), sems("carried", 2), sem("tot_out")

        y_part, count_max = sem("y_part"), sem("count_max")
        TRIG_OPS = 8
        PC2 = TRIG_OPS * NBLK
        ROOT_OPS = 11
        x_in, a_in, stored = sems("x_in", NRING), sems("a_in", NRING), sems("stored", NRING)
        nturned, nturned_out, sc_ready = sem("nturned"), sem("nturned_out"), sem("sc_ready")
        std_ready, inverse_ready, gated_first = sem("std_ready"), sem("inverse_ready"), sem("gated_first")
        abs_ready, gated, pair_summed, attr_copied = sem("abs_ready"), sem("gated"), sem("pair_summed"), sem("attr_copied")
        y_stt, y_sum, stats_ready, mv_ready = sem("y_stt"), sem("y_sum"), sem("stats_ready"), sem("mv_ready")
        root_chain, shift_ready, normed = sem("root_chain"), sem("shift_ready"), sem("normed")
        gates_ready, trig_ready, sin_ready, count_ready, pool_chain = (sem("gates_ready"), sem("trig_ready"),
                                                                       sem("sin_ready"), sem("count_ready"), sem("pool_chain"))

        slot_uses = [len(range(k, NPAIR, RING)) for k in range(RING)]
        EDGE_STEADY, POOL_STEADY = (4, 96), (8, 96)
        NODE_STEADY = (NRING, 96)

        def edge_count(l, q):
            return q + (l * NPAIR + 1)

        def slot_count(l, k, turn):
            return turn + (l * slot_uses[k] + 1)

        def node_count(l, b):
            return b + (l * NBLK + 1)

        node_uses = [len(range(k, NBLK, NRING)) for k in range(NRING)]

        def node_slot(l, k, turn):
            return turn + (l * node_uses[k] + 1)

        block = ctx.enter_context(nc.Block())

        N_ROWS_IN, N_STAGE = 5, 0

        def weight_loads():
            g = lambda n: w[n]
            loads = []
            for l, L in enumerate(LAYERS):
                names = [
                    dict(fc1='L0_gnn_fcW1', fc2='L0_gnn_fcW2', s=['L0_gnn_W1_s'], v=['L0_gnn_W1_v'],
                         cs=['L0_gnn_W_sc_s'], cv=['L0_gnn_W_sc_v'], l2s=['L0_gnn_W2_s'], l2v=['L0_gnn_W2_v'],
                         ex='L0_gnn_W3'),
                    dict(fc1='L1_gnn_W_fc1', fc2='L1_gnn_W_fc2', s=['L1_gnn_W_l1_0'], v=['L1_gnn_W_l1_1'],
                         cs=['L1_gnn_W_si0'], cv=['L1_gnn_W_si1'], l2s=['L1_gnn_W_l2_00', 'L1_gnn_W_l2_10'],
                         l2v=['L1_gnn_W_l2_01', 'L1_gnn_W_l2_11'], ex=None),
                    dict(fc1='L2_gnn_Wfc1', fc2='L2_gnn_Wfc2', s=['L2_gnn_Wl1_0'], v=['L2_gnn_Wl1_1'],
                         cs=['L2_gnn_Wsc0'], cv=['L2_gnn_Wsc1'], l2s=['L2_gnn_Wl2_s'], l2v=['L2_gnn_Wl2_v'],
                         ex='L2_gnn_Wa'),
                    dict(fc1='L3_gnn_W_fc1', fc2='L3_gnn_W_fc2', s=['L3_gnn_Ws_l1_a', 'L3_gnn_Ws_l1_c'],
                         v=['L3_gnn_Wv_l1_a', 'L3_gnn_Wv_l1_c'], cs=['L3_gnn_Ws_sc_a', 'L3_gnn_Ws_sc_c'],
                         cv=['L3_gnn_Wv_sc_a', 'L3_gnn_Wv_sc_c'], l2s=None, l2v=None, ex=None),
                ][l]
                st = STAGE[l]
                loads.append((fc1[l][100:100 + L["rad"], :], g(names['fc1'])))
                o, f = st['fc2'], g(names['fc2'])
                for at, a, b in ((0, 0, 64), (64, 128, 160), (96, 64, 128), (160, 160, 192)):
                    loads.append((stage[0:L["hid"], o + at:o + at + b - a], f[:, a:b]))
                for key, name in (('w1s', 's'), ('scs', 'cs'))[0:1 if l < 3 else 2]:
                    for j, n in enumerate(names[name]):
                        loads.append((stage[0:S, st[key] + j * S:st[key] + (j + 1) * S], g(n)))
                for key, name in (('w1v', 'v'), ('scv', 'cv'))[0:1 if l < 3 else 2]:
                    for j, n in enumerate(names[name]):
                        for d in range(3):
                            c = st[key] + j * 96 + d * V
                            loads.append((stage[d:d + 3 * (V - 1) + 1:3, c:c + V], g(n)))
                if l < 3:
                    loads.append((stage[0:S, st['head']:st['head'] + S], g(names['cs'][0])))
                    for d in range(3):
                        of = g(names['cv'][0])
                        cut = -(-(64 - d) // 3)
                        c, row = st['head'] + S + d * V, S + d
                        loads.append((stage[row:row + 3 * (cut - 1) + 1:3, c:c + V], of[0:cut, :]))
                        c, row = st['tail'] + d * V, 96 + 3 * cut + d - 64
                        loads.append((stage[row:row + 3 * (V - cut - 1) + 1:3, c:c + V], of[cut:V, :]))
                    o, row = st['w2'], 1
                    for n in names['l2s']:
                        loads.append((stage[row:row + g(n).shape[0], o + 2:o + 2 + S], g(n)))
                        row += g(n).shape[0]
                    row = 1
                    for n in names['l2v']:
                        for d in range(3):
                            c = o + 2 + S + d * V
                            loads.append((stage[row:row + g(n).shape[0], c:c + V], g(n)))
                        row += g(n).shape[0]
                    if names['ex']:
                        loads.append((stage[1:97, o:o + 1], g(names['ex'])))
                    if l == 2:
                        loads.append((stage[97:98, o + 1:o + 2], ones[0:1, 0:1]))
                else:
                    o = st['l2']
                    for j, n in enumerate(('L3_gnn_Ws_l2_a', 'L3_gnn_Ws_l2_c', 'L3_gnn_Wv_l2_a', 'L3_gnn_Wv_l2_c')):
                        loads.append((stage[0:96, o + 96 * j:o + 96 * j + 96], g(n)))
                    loads.append((stage[0:96, o + 384:o + 448], g('L3_gnn_Ws_l3')))
                    loads.append((stage[0:96, o + 448:o + 480], g('L3_gnn_Wv_l3')))
            return loads

        STAGE, col = [], 0
        for l, L in enumerate(LAYERS):
            st = {}
            for key, width in (('fc2', 192), ('w1s', L["groups"] * S), ('w1v', L["groups"] * 96),
                               ('scs' if l == 3 else 'head', 2 * S if l == 3 else F),
                               ('scv' if l == 3 else 'tail', 2 * 96 if l == 3 else 96),
                               ('w2', AW) if l < 3 else ('l2', 480 + 4 * MR)):
                st[key] = col
                col += width
            STAGE.append(st)
        assert col <= 4096
        LOADS = weight_loads()
        flat = lambda ap: ap.rearrange("e c -> (e c)")
        pair_rows = lambda ap: ap.rearrange("(q e) c -> q (e c)", q=NPAIR)

        def edge_rows_before(ap):
            return flat(ap)[510:510 + 512 * (NPAIR - 1)].rearrange("(q c) -> q c", c=512)

        @block.sync
        def _(sp):
            sp.dma_start(pairs0, pair_rows(pairs)).then_inc(given_in, 16)
            sp.wait_ge(filled, 1)
            sp.dma_start(prev0[1:NPAIR, :], edge_rows_before(pairs)).then_inc(given_in, 16)
            sp.dma_start(prev0[0:1, 2:512], pair_rows(pairs)[0:1, 0:510]).then_inc(given_in, 16)
            sp.wait_ge(records_ready, 1)
            sp.wait_ge(rows_blank, 1)
            sp.dma_start(pairs1, pair_rows(rec_pairs)).then_inc(rows_in, 16)
            sp.dma_start(prev1[1:NPAIR, :], edge_rows_before(rec_pairs)).then_inc(rows_in, 16)
            sp.dma_start(prev1[0:1, 2:512], pair_rows(rec_pairs)[0:1, 0:510]).then_inc(rows_in, 16)
            sp.dma_start(next1[0:NPAIR - 1, :], pair_rows(rec_pairs)[1:NPAIR, 0:2]).then_inc(rows_in, 16)
            sp.dma_start(attr_rows, pair_rows(rec_attr)).then_inc(attr_in0, 16)
            sp.wait_ge(chain, CHAIN_DST)
            sp.dma_start(dst_row.rearrange("o (q e) -> (o q) e", q=NPAIR), dst1).then_inc(dst_out, 16)
            sp.wait_ge(dst_out, 16)
            sp.wait_ge(meta_ready, 1)
            for c in range(6, -1, -1):
                n = EP // 7
                sp.dma_start(same_all[:, c * n:(c + 1) * n], dst_row[:, c * n:(c + 1) * n].to_broadcast([P, n]))\
                    .then_inc(dst_in_first if c == 6 else dst_in, 16)

            for l in range(4):
                L = LAYERS[l]

                def edge_loads(q, k, turn):
                    if within(q, 0, NPAIR):
                        pair = (NPAIR - 1) - q
                        if not isinstance(q, int):
                            pair = sp.snap(pair)
                        ea = rec_attr.rearrange("(q t p) c -> p q t c", t=2, p=P)
                        wait(sp, msg_ready, edge_count(l, q - RING))
                        alone(sp, passed["sp"])
                        sp.dma_start(meta[:, k, :], meta_all[:, bass.ds(pair, 1), :]
                                     .rearrange("p o c -> p (o c)")).then_inc(meta_in[k], 16)
                        sp.dma_start(xg[:, k, :, XW:XW + L["rad"]],
                                     ea[:, bass.ds(pair, 1), :, L["at"]:L["at"] + L["rad"]]
                                     .rearrange("p o t c -> p (o t) c")).then_inc(ea_in[k], 16)
                    if within(q, 4, NPAIR + 4):
                        pair = (NPAIR + 3) - q
                        if not isinstance(q, int):
                            pair = sp.snap(pair)
                        if l or within(q, 8, NPAIR + 8):
                            kk, tt = back(k, turn, 8)
                            wait(sp, spread[kk], slot_count(l, kk, tt) * 32)
                            alone(sp, passed["sp"])
                        sp.dma_start(sidx[:, k, :], meta_all[:, bass.ds(pair, 1), 2:4]
                                     .rearrange("p o c -> p (o c)")).then_inc(sidx_in[k], 16)

                if l == 0:
                    sp.wait_ge(meta_ready, 1)
                z3 = flat(agg3).rearrange("(c p n) -> c p n", c=NBLK, p=P)

                def edge_loads_and_zeros(q, k, turn):
                    edge_loads(q, k, turn)
                    if l == 1 and within(q, 0, NBLK):
                        c = q if isinstance(q, int) else sp.snap(q)
                        sp.dma_start(z3[bass.ds(c, 1)].rearrange("o p n -> (o p) n"), zeros[:, 0:BT * AW3]).then_inc(zeroed3, 16)

                steps(sp, 0, NPAIR + 4, POOL_STEADY, edge_loads_and_zeros)

                xrows = xtab[l].rearrange("(b p t) c -> b p (t c)", p=P, t=BT)
                arows = (agg if l < 3 else agg3).rearrange("(b p t) c -> b p (t c)", p=P, t=BT)
                abuf = an if l < 3 else an3
                for k in range(RING):
                    sp.wait_ge(spread[k], 32 * slot_uses[k] * (l + 1))

                def node_loads(b, k, turn):
                    if not isinstance(b, int):
                        b = sp.snap(b)
                    wait(sp, y_sum, node_count(l, b - NRING))
                    if l < 3 or isinstance(b, int) and b < NRING:
                        wait(sp, attr_copied, node_count(l, b - NRING))
                    alone(sp, passed["sp"])
                    sp.dma_start(xn[:, k].rearrange("p t c -> p (t c)"),
                                 xrows[bass.ds(b, 1)].rearrange("o p c -> (o p) c")).then_inc(x_in[k], 16)
                    sp.dma_start(abuf[:, k].rearrange("p t c -> p (t c)"),
                                 arows[bass.ds(b, 1)].rearrange("o p c -> (o p) c")).then_inc(a_in[k], 16)

                steps(sp, 0, NBLK, NODE_STEADY, node_loads, NRING)
            for k in range(NRING):
                sp.wait_ge(stored[k], 16 * 4 * node_uses[k])
            sp.wait_ge(zeroed3, 16 * NBLK)

        @block.gpsimd
        def _(gp):
            gp.memset(ident[:, :], 0.0).then_inc(ident_a, 1)
            gp.wait_ge(ident_a, 1)
            gp.affine_select(out=ident[:, :], in_=ident[:, :], compare_op=ALU.not_equal, fill=1.0, base=0,
                             pattern=[[-1, P]], channel_multiplier=1).then_inc(ident_ready, 1)
            gp.dma_start(rec_pairs.rearrange("(q e) c -> q (e c)", q=P), pairs.rearrange("(q e) c -> q (e c)", q=P)).then_inc(copied, 16)
            gp.dma_start(rec_attr.rearrange("(q e) c -> q (e c)", q=P), eattr.rearrange("(q e) c -> q (e c)", q=P)).then_inc(copied, 16)
            gp.wait_ge(copied, 32)
            gp.wait_ge(flag_ready, 1)
            unsorted = gp.value_load(flag, min_val=0, max_val=1)
            with gp.If(unsorted > 0):
                gp.iota(sort_a.bitcast(i32), pattern=[[1, SORT_COLS]], base=0, channel_multiplier=0).then_inc(iota_ready, 1)
                gp.iota(sort_s[:, 0:1].bitcast(i32), pattern=[[0, 1]], base=0, channel_multiplier=1).then_inc(iota_ready, 1)
                gp.dma_start(dst_row0.rearrange("o (q e) -> (o q) e", q=NPAIR), dst0).then_inc(sort_dma, 16)
                gp.wait_ge(sort_dma, 16)
                gp.dma_start(same_all[:, :].rearrange("p (a n) -> p a n", n=EP // 4),
                             dst_row0.rearrange("o (a n) -> o a n", n=EP // 4).to_broadcast([P, 4, EP // 4])).then_inc(bcast_in, 16)
                gp.sem_inc(ranks_free, 1)
                with gp.Fori(0, NT) as t:
                    gp.dma_start(sort_pair, pairs[bass.ds(t * P, P), :]).then_inc(sort_io, 16)
                    gp.dma_start(sort_attr, eattr[bass.ds(t * P, P), :]).then_inc(sort_io, 16)
                    gp.wait_ge(sort_io, t * 32 + 32)
                    gp.wait_ge(pos_ready, t + 1)
                    alone(gp, passed["gp"])
                    at = bass.IndirectOffsetOnAxis(ap=sort_s[:, 8:9].bitcast(i32), axis=0)
                    gp.indirect_dma_start(rec_pairs, at, sort_pair, None).then_inc(scattered, 16)
                    gp.indirect_dma_start(rec_attr, at, sort_attr, None).then_inc(scattered, 16)
                    gp.wait_ge(scattered, t * 32 + 32)
                    gp.sem_inc(ranks_free, 1)
            gp.engine_nop().then_inc(records_ready, 1)
            gp.wait_ge(meta_ready, 1)
            for l in range(4):
                def edge_moves(q, k, turn):
                    if within(q, 0, NPAIR):
                        gp.wait_ge(meta_in[k], slot_count(l, k, turn) * 16)
                        wait(gp, turned, edge_count(l, q - RING))
                        alone(gp, passed["gp"])
                        for t in range(2):
                            at = bass.IndirectOffsetOnAxis(ap=meta[:, k, t:t + 1].bitcast(i32), axis=0)
                            gp.indirect_dma_start(xg[:, k, t, 0:XW], None, xtab[l], at).then_inc(gathered[k], 16)
                    if within(q, 6, NPAIR + 6):
                        kk, tt = back(k, turn, 6)
                        if l == 0 and isinstance(q, int) and q == 6:
                            gp.wait_ge(zeroed, 16 * (NP * AW // (P * 2025)))
                        gp.wait_ge(tot_out, edge_count(l, q - 6))
                        gp.wait_ge(sidx_in[kk], slot_count(l, kk, tt) * 16)
                        alone(gp, passed["gp"])
                        for t in range(2):
                            at = bass.IndirectOffsetOnAxis(ap=sidx[:, kk, t:t + 1].bitcast(i32), axis=0)
                            gp.indirect_dma_start(agg if l < 3 else agg3, at, tot[:, kk, t, 0:aw[l]], None,
                                                  bounds_check=NP - 1, oob_is_err=False).then_inc(spread[kk], 16)

                if l == 3:
                    gp.wait_ge(zeroed3, 16 * NBLK)
                for k in range(NRING):
                    wait(gp, stored[k], l * node_uses[k] * 16)
                steps(gp, 0, NPAIR + 6, POOL_STEADY, edge_moves)

                G = LAYERS[l]["groups"]
                to = out if l == 3 else xtab[l + 1]
                xrows = to.rearrange("(b p t) c -> b p t c", p=P, t=BT)

                def link(ins, at):
                    ins.then_inc(pool_chain, 1)
                    gp.wait_ge(pool_chain, at)
                    alone(gp, passed["gp"])

                def bring_in(b, k, turn):
                    angle, turns, rounded, less, rest, clipped = (trig[:, k, n] for n in range(6))
                    x0 = xn[:, k, :, F]
                    at = b * TRIG_OPS
                    wait(gp, y_sum, b + (1 - NRING))
                    gp.wait_ge(x_in[k], node_slot(l, k, turn) * 16)
                    gp.wait_ge(a_in[k], node_slot(l, k, turn) * 16)
                    alone(gp, passed["gp"])
                    link(gp.tensor_tensor(angle, an[:, k, :, 0], x0, ALU.mult), at + 1)
                    link(gp.tensor_scalar(turns, angle, float(0.5 / np.pi), ROUND, ALU.mult, ALU.add), at + 2)
                    link(gp.tensor_scalar(rounded, turns, ROUND, None, ALU.subtract), at + 3)
                    link(gp.tensor_scalar(turns, rounded, TWO_PI_HI, None, ALU.mult), at + 4)
                    link(gp.tensor_tensor(less, angle, turns, ALU.subtract), at + 5)
                    link(gp.tensor_scalar(turns, rounded, TWO_PI_LO, None, ALU.mult), at + 6)
                    link(gp.tensor_tensor(rest, less, turns, ALU.subtract), at + 7)
                    link(gp.tensor_scalar(clipped, rest, 3.1415925, -3.1415925, ALU.min, ALU.max), at + 8)
                    gp.engine_nop().then_inc(trig_ready, 1)

                def make_gates(b, k, turn):
                    gp.wait_ge(x_in[k], node_slot(l, k, turn) * 16)
                    x0 = xn[:, k, :, F]

                    if l < 3:
                        wait(gp, stored[k], node_slot(l, k, turn - 1) * 16)
                        alone(gp, passed["gp"])
                        gp.tensor_copy(yn[:, k, :, F:XW], xn[:, k, :, F:XW]).then_inc(attr_copied, 1)
                    if l != 1:
                        wait(gp, y_sum, node_count(l, b - NRING))
                        gp.wait_ge(a_in[k], node_slot(l, k, turn) * 16)
                        alone(gp, passed["gp"])
                    if l == 0:
                        if isinstance(b, int) and b == 0:
                            bring_in(b, k, turn)
                        gp.wait_ge(sin_ready, b + 1)
                        gp.tensor_tensor(gates[:, k, :, 0], waves[:, k, 0, :], x0, ALU.mult)
                        gp.tensor_tensor(gates[:, k, :, 1], waves[:, k, 1, :], x0, ALU.mult).then_inc(gates_ready, 1)
                        if within(b, 0, NBLK - 1):
                            bring_in(b + 1, (k + 1) % NRING, turn + (k + 1) // NRING)
                    if l == 2:
                        gp.wait_ge(count_ready, b + 1)
                        alone(gp, passed["gp"])
                        at = b * 2 + PC2
                        link(gp.tensor_tensor(gates[:, k, :, 0], x0, inv_count[:, k, 1, :], ALU.mult), at + 1)
                        link(gp.tensor_tensor(gates[:, k, :, 1], gates[:, k, :, 0], gates[:, k, :, 0], ALU.mult), at + 2)
                        gp.tensor_tensor(gates[:, k, :, 0], gates[:, k, :, 1], an[:, k, :, 0], ALU.mult).then_inc(gates_ready, 1)
                    if l == 3:
                        gp.tensor_tensor(gates[:, k, :, 0], x0, xn[:, k, :, F + 2], ALU.mult)
                        gp.tensor_tensor(gates[:, k, :, 1], xn[:, k, :, F + 1], xn[:, k, :, F + 2], ALU.mult).then_inc(gates_ready, 1)
                        gp.wait_ge(gates_ready, b + (2 * NBLK + 1))
                        alone(gp, passed["gp"])
                        gp.tensor_tensor(an3[:, k, :, 0:F], an3[:, k, :, 0:F], gates[:, k, :, 0:1].to_broadcast([P, BT, F]),
                                         ALU.mult).then_inc(gated_first, 1)
                        gp.wait_ge(gated_first, b + 1)
                        gp.wait_ge(gated, b + (2 * NBLK + 1))
                        alone(gp, passed["gp"])
                        gp.tensor_tensor(an3[:, k, :, 0:F], an3[:, k, :, 0:F], an3[:, k, :, F:2 * F], ALU.add).then_inc(pair_summed, 1)

                def store_normed(b, k, turn):
                    kk, tt = back(k, turn, 5, NRING)
                    done = b - 5
                    if not isinstance(b, int):
                        done = gp.snap(done)
                    gp.wait_ge(normed, node_count(l, b - 5))
                    if l < 3:
                        gp.wait_ge(attr_copied, node_count(l, b - 5))
                    width = F if l == 3 else XW
                    gp.dma_start(xrows[bass.ds(done, 1)].rearrange("o p t c -> (o p) t c"),
                                 yn[:, kk, :, 0:width]).then_inc(stored[kk], 16)

                def node_moves(b, k, turn):
                    if l != 2 and within(b, 5, NBLK + 5):
                        store_normed(b, k, turn)
                    if within(b, 0, NBLK):
                        make_gates(b, k, turn)
                    if l == 2 and within(b, 5, NBLK + 5):
                        store_normed(b, k, turn)

                steps(gp, 0, NBLK + 5, NODE_STEADY, node_moves, NRING)

        @block.tensor
        def _(pe):
            pe.wait_ge(ident_ready, 1)
            pe.wait_ge(viol_ready, 1)
            nc.tensor.matmul(bank[0][0:1, 0:1], viol, ones[0:NPAIR, 0:1], start=True, stop=True).then_inc(viol_summed, 1)
            for t in range(2):
                last = nc.tensor.transpose(bank[1][:, t * NPAIR:(t + 1) * NPAIR], dst0[:, t * P:(t + 1) * P],
                                           ident[0:NPAIR, 0:NPAIR])
            last.then_inc(dcol_turned, 1)
            pe.wait_ge(fields_ready, 1)
            pe.wait_ge(attr_in0, 16)
            rows = attr_rows.rearrange("q (t e c) -> q t e c", t=2, c=EA)
            cols = [f[:, t * P:(t + 1) * P] for f in (src1, idx1, dst1, carry1) for t in range(2)]
            cols += [rows[:, t, :, c] for t in range(2) for c in range(4)]
            for n, c in enumerate(cols):
                o = (n % 4) * NPAIR
                last = nc.tensor.transpose(bank[2 + n // 4][:, o:o + NPAIR], c, ident[0:NPAIR, 0:NPAIR])
            last.then_inc(fields_turned, 1)
            o = STAGE[3]['l2']
            pe.wait_ge(stage_in, 16 * len(LOADS))
            for j in range(4):
                last = nc.tensor.transpose(bank[6][0:96, 96 * j:96 * j + 96], stage[0:96, o + 96 * j:o + 96 * j + 96],
                                           ident[0:96, 0:96])
            last.then_inc(l2_turned, 1)
            pe.wait_ge(l2_copied, 1)
            ot = o + 480
            for j in range(4):
                a, b = (384, 448) if j < 2 else (448, 480)
                at = (0, 64, 128, 160)[j]
                last = nc.tensor.matmul(bank[7][0:MR, at:at + b - a], stage[0:96, ot + MR * j:ot + MR * (j + 1)],
                                        stage[0:96, o + a:o + b], start=True, stop=True)
            last.then_inc(l2_product, 1)
            pe.wait_ge(weights_ready, 1)
            pe.wait_ge(meta_ready, 1)

            for l in range(4):
                L = LAYERS[l]
                G = L["groups"]
                fb = [bank[3], bank[3]] if G == 1 else [bank[3], bank[4]]
                fo = [0, F] if G == 1 else [0, 0]
                tb = [bank[4], bank[7]] if G == 1 else [bank[7], bank[7]]

                def edge_products(q, k, turn):
                    k2 = k % 2
                    if not isinstance(q, int):
                        here = [pe.snap(((NPAIR + 1 - q) * 2 + t) * P) for t in range(2)]
                    else:
                        here = [((NPAIR + 1 - q) * 2 + t) * P for t in range(2)]
                    has_new, has_old = within(q, 0, NPAIR), within(q, 2, NPAIR + 2)
                    if has_new:
                        pe.wait_ge(gathered[k], slot_count(l, k, turn) * 32)
                        pe.wait_ge(ea_in[k], slot_count(l, k, turn) * 16)
                        wait(pe, turned_out, edge_count(l, q - 1))
                        for c, a in ((0, 0), (1, S)):
                            for t in range(2):
                                last = nc.tensor.transpose(bank[0][:, (2 * c + t) * P:(2 * c + t + 1) * P],
                                                           xg[:, k, t, a:a + P], ident[:, :])
                        last.then_inc(turned, 1)
                    if has_old:
                        pe.wait_ge(msg_ready, edge_count(l, q - 2))
                        if l == 0:
                            pe.wait_ge(same_ready, (q - 1) * 2)
                        for t in (1, 0):
                            wait(pe, summed_out[t], edge_count(l, q - 3))
                            alone(pe, passed["pe"])
                            for c in range(4):
                                last = nc.tensor.matmul(bank[5 + t][0:MR, c * P:(c + 1) * P], msg[:, k2, t, c, :],
                                                        same_all[:, bass.ds(here[t], P)], start=True, stop=True)
                            last.then_inc(summed[t], 1)
                    if has_new:
                        pe.wait_ge(turned_out, edge_count(l, q))
                        wait(pe, h_act, edge_count(l, q - 1))
                        nc.tensor.matmul(bank[1][0:L["hid"], 0:256], fc1[l][96:128, :], xT[96:128, k2, 256:512],
                                         start=True, stop=True).then_inc(h_ready, 1)

                    def second_map(t):
                        pe.wait_ge(summed_out[t], edge_count(l, q - 2))
                        if t == 0:
                            pe.wait_ge(carried[0], edge_count(l, q - 2))
                        else:
                            wait(pe, carried[1], edge_count(l, q - 3))
                        if G == 1:
                            wait(pe, tot_out, edge_count(l, q - 3))
                        elif t == 1:
                            wait(pe, tot_out, edge_count(l, q - 3))
                        else:
                            pe.wait_ge(carried_tot, edge_count(l, q - 2))
                        head = 2 + S if G == 1 else 2 * S
                        nc.tensor.matmul(tb[t][:, 0:head], aggT[:, t, 0:P], w2[l][:, t, 0:head], start=True, stop=True)
                        for d in range(3):
                            a, b = head + d * G * V, head + (d + 1) * G * V
                            last = nc.tensor.matmul(tb[t][:, a:b], aggT[:, t, (d + 1) * P:(d + 2) * P],
                                                    w2[l][:, t, a:b], start=True, stop=True)
                        last.then_inc(tot_ready[t], 1)

                    if has_old:
                        second_map(1)
                    if has_new:
                        wait(pe, msg_ready, edge_count(l, q - 1))
                        for t in range(2):
                            both = lambda ap: ap.rearrange("p (g c) -> p g c", g=G)
                            to = both(fb[t][:, fo[t]:fo[t] + G * F])
                            nc.tensor.matmul(to[:, :, 0:S], xT[0:S, k2, t * P:(t + 1) * P], both(w1s[l][:, :]),
                                             start=True, stop=True)
                            last = nc.tensor.matmul(to[:, :, S:F], xT[0:96, k2, (2 + t) * P:(3 + t) * P],
                                                    both(w1v[l][:, :]), start=True, stop=True)
                        last.then_inc(f_ready, 1)
                        pe.wait_ge(h_act, edge_count(l, q))
                        for t in range(2):
                            last = nc.tensor.matmul(bank[2][:, t * 192:(t + 1) * 192], hT[0:L["hid"], k2, t * P:(t + 1) * P],
                                                    fc2[l][:, :], start=True, stop=True)
                        last.then_inc(w_ready, 1)
                    if has_old:
                        second_map(0)

                steps(pe, 0, NPAIR + 2, EDGE_STEADY, edge_products)

                pe.wait_ge(tot_out, edge_count(l, NPAIR - 1))
                pe.wait_ge(msg_ready, edge_count(l, NPAIR - 1))
                if l == 3:
                    pe.wait_ge(carried_tot, edge_count(l, NPAIR - 1))

                def node_products(b, k, turn):
                    base = b * 2 + 2 * l * NBLK
                    kk, tt = back(k, turn, 1, NRING)
                    has_new, has_old = within(b, 0, NBLK), within(b, 1, NBLK + 1)
                    if has_new:
                        pe.wait_ge(x_in[k], node_slot(l, k, turn) * 16)
                    for d in range(2):
                        if has_new:
                            wait(pe, nturned_out, base + (d - 1))
                            alone(pe, passed["pe"])
                            rows = P if G == 1 else 96
                            for c, a in ((0, 0), (1, F - rows)):
                                for t in range(2):
                                    last = nc.tensor.transpose(bank[d][0:rows, (2 * c + t) * P:(2 * c + t + 1) * P],
                                                               xn[:, k, 2 * d + t, a:a + rows], ident[:, :])
                            last.then_inc(nturned, 1)
                        if not has_old:
                            continue
                        pe.wait_ge(nturned_out, base + (d - 1))
                        if l == 1:
                            pe.wait_ge(a_in[kk], node_slot(l, kk, tt) * 16)
                        wait(pe, y_stt, base + (d - (7 if G == 1 else 4)))
                        for t in range(2):
                            ob = bank[2 + (2 * kk + d) % 6] if G == 1 else bank[2 + (4 * kk + 2 * d + t) % 6]
                            head, tail = xT[:, d, t * P:(t + 1) * P], xT[:, d, (2 + t) * P:(3 + t) * P]
                            if G == 1:
                                nc.tensor.matmul(ob[:, t * F:(t + 1) * F], head, sc_head[l][:, :], start=True, stop=False)
                                last = nc.tensor.matmul(ob[:, t * F + S:(t + 1) * F], tail[96:P, :], sc_tail[l][96:P, :],
                                                        start=False, stop=l != 1)
                                if l == 1:
                                    last = nc.tensor.matmul(ob[:, t * F:(t + 1) * F], ident[:, :], an[:, kk, 2 * d + t, 2:AW],
                                                            start=False, stop=True)
                            else:
                                both = lambda ap: ap.rearrange("p (g c) -> p g c", g=G)
                                to = both(ob[:, 0:G * F])
                                nc.tensor.matmul(to[:, :, 0:S], head[0:S, :], both(scs3[:, :]), start=True, stop=True)
                                last = nc.tensor.matmul(to[:, :, S:F], tail[0:96, :], both(scv3[:, :]), start=True, stop=True)
                        last.then_inc(sc_ready, 1)

                steps(pe, 0, NBLK + 1, NODE_STEADY, node_products, NRING)
                pe.wait_ge(y_stt, 2 * NBLK * (l + 1))

        @block.scalar
        def _(act):
            act.wait_ge(stage_zero, 1)
            with nc.allow_non_contiguous_dma(reason="one column of weights"):
                for to, of in LOADS:
                    act.dma_start(to, of).then_inc(stage_in, 16)
            zrows = flat(agg).rearrange("(c p n) -> c p n", p=P, n=2025)
            for c in range(NP * AW // (P * 2025)):
                act.dma_start(zrows[c], zeros[:, :]).then_inc(zeroed, 16)
            act.wait_ge(meta_ready, 1)
            act.wait_ge(weights_ready, 1)
            for l in range(4):
                L = LAYERS[l]
                G = L["groups"]
                fb = [bank[3], bank[3]] if G == 1 else [bank[3], bank[4]]
                tb = [bank[4], bank[7]] if G == 1 else [bank[7], bank[7]]

                def edge_copies(q, k, turn):
                    k2 = k % 2
                    has_new, has_old = within(q, 0, NPAIR), within(q, 2, NPAIR + 2)
                    if has_new:
                        act.wait_ge(turned, edge_count(l, q))
                        wait(act, f_ready, edge_count(l, q - 2))
                        nc.scalar.activation(xT[:, k2, :], bank[0][:, :], ACT.Copy).then_inc(turned_out, 1)
                    if has_old:
                        act.wait_ge(summed[1], edge_count(l, q - 2))
                        wait(act, tot_ready[1], edge_count(l, q - 3))
                        nc.scalar.activation(aggT[:, 1, :], bank[6][0:MR, :], ACT.Copy).then_inc(summed_out[1], 1)
                    if has_new:
                        act.wait_ge(h_ready, edge_count(l, q))
                        wait(act, w_ready, edge_count(l, q - 2))
                        nc.scalar.activation(hT[0:L["hid"], k2, :], bank[1][0:L["hid"], 0:256],
                                             ACT.Silu if L["silu"] else ACT.Relu, scale=L["hs"]).then_inc(h_act, 1)

                    def totals(t):
                        kk, tt = back(k, turn, 2)
                        act.wait_ge(tot_ready[t], edge_count(l, q - 2))
                        nc.scalar.activation(w2[l][0:1, 1 - t, :], tb[t][0:1, 0:aw[l]], ACT.Copy).then_inc(carried[1 - t], 1)
                        if t == 1 and (l or within(q, 6, NPAIR + 6)):
                            k6, t6 = back(k, turn, 6)
                            wait(act, spread[k6], slot_count(l, k6, t6) * 32)
                        if G == 1:
                            nc.scalar.activation(tot[:, kk, t, 0:2 + S], tb[t][:, 0:2 + S], ACT.Copy)
                            last = nc.scalar.activation(tot[:, kk, t, 2 + S:AW].rearrange("p (v d) -> p v d", d=3),
                                                        tb[t][:, 2 + S:AW].rearrange("p (d v) -> p v d", d=3), ACT.Copy)
                        else:
                            to = tot[:, kk, t, :].rearrange("p (g c) -> p g c", g=2)
                            nc.scalar.activation(to[:, :, 0:S], tb[t][:, 0:2 * S].rearrange("p (g c) -> p g c", g=2), ACT.Copy)
                            of = tb[t][:, 2 * S:AW3].rearrange("p (d g v) -> p g v d", d=3, g=2)
                            for g in range(2):
                                last = nc.scalar.activation(to[:, g, S:F].rearrange("p (v d) -> p v d", d=3),
                                                            of[:, g], ACT.Copy)
                        last.then_inc(tot_out if t == 0 else carried_tot, 1)

                    if has_old:
                        totals(1)
                    if has_new and G == 2:
                        act.wait_ge(f_ready, edge_count(l, q))
                        wait(act, msg_ready, edge_count(l, q - 2))
                        for t in range(2):
                            last = nc.scalar.activation(fsum[:, k2, t, :], fb[t][:, 0:F], ACT.Copy,
                                                        scale=xg[:, k, t, F:F + 1])
                        last.then_inc(fa_out, 1)
                    if has_old:
                        totals(0)

                steps(act, 0, NPAIR + 2, EDGE_STEADY, edge_copies)

                def sines(b, k):
                    act.wait_ge(trig_ready, b + 1)
                    wait(act, gates_ready, b + (1 - NRING))
                    nc.scalar.activation(trig[:, k, 0], trig[:, k, 5], ACT.Abs).then_inc(abs_ready, 1)
                    nc.scalar.activation(waves[:, k, 0, :], trig[:, k, 5], ACT.Sin)
                    act.wait_ge(abs_ready, b + 1)
                    nc.scalar.activation(waves[:, k, 1, :], trig[:, k, 0], ACT.Sin, scale=-1.0,
                                         bias=half_pi[:, :]).then_inc(sin_ready, 1)

                def node_copies(b, k, turn):
                    if within(b, 0, NBLK):
                        base = b * 2 + 2 * l * NBLK
                        for d in range(2):
                            act.wait_ge(nturned, base + (d + 1))
                            wait(act, sc_ready, base + (d - 1))
                            rows = P if G == 1 else 96
                            nc.scalar.activation(xT[0:rows, d, :], bank[d][0:rows, :], ACT.Copy).then_inc(nturned_out, 1)
                        if l == 0 and isinstance(b, int) and b == 0:
                            sines(b, k)
                    if l != 1 and within(b, 0, NBLK):
                        act.wait_ge(gates_ready, b + {0: 1, 2: NBLK + 1, 3: 2 * NBLK + 1}[l])
                        alone(act, passed["act"])
                        for j in range(BT):
                            sums = an[:, k, j, 2:AW] if G == 1 else an3[:, k, j, F:2 * F]
                            last = nc.scalar.activation(sums, sums, ACT.Copy, scale=gates[:, k, j, G - 1:G])
                        last.then_inc(gated, 1)
                    if l and within(b, 2, NBLK + 2):
                        kk, tt = back(k, turn, 2, NRING)
                        act.wait_ge(mv_ready, node_count(l, b - 2))
                        nc.scalar.activation(std[:, kk, :], mv[:, kk, :, 1], ACT.Sqrt, bias=eps[:, :]).then_inc(std_ready, 1)
                    if within(b, 4, NBLK + 4):
                        kk, tt = back(k, turn, 4, NRING)
                        act.wait_ge(shift_ready, node_count(l, b - 4))
                        for t in range(BT):
                            last = nc.scalar.activation(yn[:, kk, t, 0:F], yn[:, kk, t, 0:F], ACT.Identity,
                                                        bias=shift[:, kk, t:t + 1], scale=rstd[:, kk, t:t + 1])
                        last.then_inc(normed, 1)
                    if l == 0 and within(b, 0, NBLK - 1):
                        sines(b + 1, (k + 1) % NRING)

                steps(act, 0, NBLK + 4, NODE_STEADY, node_copies, NRING)

        @block.vector
        def _(dve):
            count = [0]

            def link(ins):
                count[0] += 1
                ins.then_inc(chain, 1)
                dve.wait_ge(chain, count[0])

            nc.vector.memset(prev0, -1)
            nc.vector.memset(ones[:, :], 1.0)
            nc.vector.memset(half_pi[:, :], float(np.pi / 2))
            nc.vector.memset(eps[:, :], EPS)
            link(nc.vector.memset(zeros[:, :], 0.0))
            dve.engine_nop().then_inc(filled, 1)
            link(nc.vector.memset(stage, 0.0))
            for l in range(4):
                nc.vector.memset(fc1[l][96:128, :], 0.0)
            nc.vector.memset(xg[:, :, :, :], 0.0)
            nc.vector.memset(msg[:, :, :, :, MR - 1:MR], 1.0)
            link(nc.vector.memset(meta_all[:, :, 14:16], 0.0))
            dve.engine_nop().then_inc(stage_zero, 1)
            dve.wait_ge(given_in, 48)
            nc.vector.tensor_copy(dst0, pairs0.rearrange("q (e c) -> q e c", c=2)[:, :, 1])
            link(nc.vector.tensor_copy(prv0, prev0.rearrange("q (e c) -> q e c", c=2)[:, :, 1]))
            link(nc.vector.tensor_tensor(less0, dst0, prv0, ALU.is_lt))
            nc.vector.tensor_reduce(viol, less0, AX.X, ALU.max).then_inc(viol_ready, 1)
            dve.wait_ge(viol_summed, 1)
            nc.vector.tensor_scalar(flag, bank[0][0:1, 0:1], 0.5, None, ALU.is_gt).then_inc(flag_ready, 1)
            dve.wait_ge(dcol_turned, 1)
            link(nc.vector.tensor_copy(dcol0.rearrange("p q t -> p t q"),
                                       bank[1][:, 0:2 * NPAIR].rearrange("p (t q) -> p t q", t=2)))
            dve.wait_ge(flag_ready, 1)
            unsorted = dve.value_load(flag, min_val=0, max_val=1)
            with dve.If(unsorted > 0):
                dve.wait_ge(iota_ready, 2)
                edge, rank, lesser, equal, start = (sort_s[:, c:c + 1] for c in (1, 2, 3, 4, 5))
                nc.vector.tensor_copy(sort_iota, sort_a.bitcast(i32)).then_inc(sort_chain, 1)
                nc.vector.tensor_copy(edge, sort_s[:, 0:1].bitcast(i32)).then_inc(sort_chain, 1)
                dve.wait_ge(sort_chain, 2)
                dve.wait_ge(bcast_in, 16)
                dall = dcol0.rearrange("p q t -> p (q t)")
                CH = EP // SORT_COLS
                per = 4 + CH * 7

                with dve.Fori(0, NT) as t:
                    n = [0]

                    def then(ins, at):
                        ins.then_inc(sort_chain, 1)
                        dve.wait_ge(sort_chain, at)
                        alone(dve, passed["dve"])

                    b0 = t * per + 2
                    then(nc.vector.tensor_copy(sort_s[:, 6:7], dall[:, bass.ds(t, 1)]), b0 + 1)
                    then(nc.vector.memset(rank, 0.0), b0 + 2)
                    then(nc.vector.tensor_copy(start, edge), b0 + 3)
                    with dve.Fori(0, CH) as c:
                        b1 = t * per + c * 7 + 5
                        cols = same_all[:, bass.ds(c * SORT_COLS, SORT_COLS)]
                        then(nc.vector.tensor_scalar(sort_a, cols, sort_s[:, 6:7], None, ALU.is_lt), b1 + 1)
                        then(nc.vector.tensor_reduce(lesser, sort_a, AX.X, ALU.add), b1 + 2)
                        then(nc.vector.tensor_scalar(sort_b, cols, sort_s[:, 6:7], None, ALU.is_equal), b1 + 3)
                        then(nc.vector.scalar_tensor_tensor(out=sort_a, in0=sort_iota, scalar=start, in1=sort_b,
                                                            op0=ALU.is_lt, op1=ALU.mult), b1 + 4)
                        then(nc.vector.tensor_reduce(equal, sort_a, AX.X, ALU.add), b1 + 5)
                        then(nc.vector.scalar_tensor_tensor(out=rank, in0=lesser, scalar=equal, in1=rank,
                                                            op0=ALU.add, op1=ALU.add), b1 + 6)
                        then(nc.vector.tensor_scalar(start, start, float(SORT_COLS), None, ALU.subtract), b1 + 7)
                    dve.wait_ge(ranks_free, t + 1)
                    nc.vector.tensor_copy(sort_s[:, 8:9].bitcast(i32), rank).then_inc(pos_ready, 1)
                    then(nc.vector.tensor_scalar(edge, edge, float(P), None, ALU.add), t * per + (per + 2))

            dve.wait_ge(records_ready, 1)
            nc.vector.memset(prev1, -1)
            nc.vector.memset(next1, -1)
            link(nc.vector.memset(carry1, 0.0))
            dve.engine_nop().then_inc(rows_blank, 1)
            dve.wait_ge(rows_in, 64)
            two = lambda ap: ap.rearrange("q (e c) -> q e c", c=2)
            nc.vector.tensor_copy(dst1, two(pairs1)[:, :, 1])
            nc.vector.tensor_copy(src1, two(pairs1)[:, :, 0])
            nc.vector.tensor_copy(nxt1, next1[:, 1:2])
            link(nc.vector.tensor_copy(prv1, two(prev1)[:, :, 1]))
            assert count[0] == CHAIN_DST
            link(nc.vector.tensor_tensor(same1, dst1, prv1, ALU.is_equal))
            nc.vector.scalar_tensor_tensor(out=idx1, in0=same1, scalar=FAR, in1=dst1, op0=ALU.mult, op1=ALU.add)
            nc.vector.tensor_tensor(carry1[:, 127:128], dst1[:, 127:128], dst1[:, 128:129], ALU.is_equal)
            link(nc.vector.tensor_tensor(carry1[:, 255:256], dst1[:, 255:256], nxt1, ALU.is_equal))
            dve.engine_nop().then_inc(fields_ready, 1)
            dve.wait_ge(fields_turned, 1)
            four = lambda b: b[:, 0:4 * NPAIR].rearrange("p (f q) -> p f q", f=4)
            by_field = lambda ap: ap.rearrange("p q f -> p f q")
            nc.vector.tensor_copy(by_field(meta_all[:, :, 0:4].bitcast(i32)), four(bank[2]))
            nc.vector.tensor_copy(by_field(dst_col[:, :, :]), four(bank[3])[:, 0:2])
            nc.vector.tensor_copy(by_field(meta_all[:, :, 4:6]), four(bank[3])[:, 2:4])
            nc.vector.tensor_copy(by_field(meta_all[:, :, 6:10]), four(bank[4]))
            link(nc.vector.tensor_copy(by_field(meta_all[:, :, 10:14]), four(bank[5])))
            dve.engine_nop().then_inc(meta_ready, 1)
            dve.wait_ge(stage_in, 16 * len(LOADS))
            scaled = lambda to, of, c: nc.vector.tensor_scalar(to, of, float(c), None, ALU.mult)
            for l, L in enumerate(LAYERS):
                st, hid, G = STAGE[l], L["hid"], L["groups"]
                scaled(fc2[l][:, 0:160], stage[0:hid, st['fc2']:st['fc2'] + 160], L["w"])
                scaled(fc2[l][:, 160:192], stage[0:hid, st['fc2'] + 160:st['fc2'] + 192], L["w"] * R3)
                scaled(w1s[l][:, :], stage[0:S, st['w1s']:st['w1s'] + G * S], L["fs"])
                scaled(w1v[l][:, :], stage[0:96, st['w1v']:st['w1v'] + G * 96], L["fv"])
                mixed = lambda to, of: scaled(to.rearrange("p (v d) -> p v d", d=3),
                                              of.rearrange("p (d v) -> p v d", d=3), L["scv"])
                if l < 3:
                    scaled(sc_head[l][:, 0:S], stage[:, st['head']:st['head'] + S], L["sc"])
                    mixed(sc_head[l][:, S:F], stage[:, st['head'] + S:st['head'] + F])
                    mixed(sc_tail[l][96:P, :], stage[96:P, st['tail']:st['tail'] + 96])
                else:
                    scaled(scs3[:, :], stage[0:S, st['scs']:st['scs'] + G * S], L["sc"])
                    for g in range(G):
                        mixed(scv3[:, g * 96:(g + 1) * 96], stage[0:96, st['scv'] + g * 96:st['scv'] + (g + 1) * 96])
                if l < 3:
                    for t in range(2):
                        o = st['w2']
                        scaled(w2[l][:, t, 0:1], stage[0:MR, o:o + 1], L["extra"])
                        scaled(w2[l][:, t, 1:2], stage[0:MR, o + 1:o + 2], 1.0)
                        scaled(w2[l][:, t, 2:AW], stage[0:MR, o + 2:o + AW], L["conv"])
            dve.wait_ge(l2_turned, 1)
            ot = STAGE[3]['l2'] + 480
            nc.vector.tensor_copy(stage[0:96, ot:ot + 4 * MR].rearrange("p (j c) -> p j c", j=4)[:, :, 1:97],
                                  bank[6][0:96, 0:384].rearrange("p (j c) -> p j c", j=4)).then_inc(l2_copied, 1)
            dve.wait_ge(l2_product, 1)
            c = LAYERS[3]["conv"]
            for t in range(2):
                scaled(w2[3][:, t, 0:128], bank[7][0:MR, 0:128], c)
                for d in range(3):
                    last = scaled(w2[3][:, t, 128 + 64 * d:192 + 64 * d], bank[7][0:MR, 128:192], c)
            link(last)
            dve.engine_nop().then_inc(weights_ready, 1)
            dflat = dst_col[:, :, :].rearrange("p q t -> p (q t)")

            for l in range(4):
                L = LAYERS[l]
                G = L["groups"]

                def edge_vectors(q, k, turn):
                    k2 = k % 2
                    if l == 0 and within(q, 0, NPAIR):
                        dve.wait_ge(dst_in_first, 16)
                        if not isinstance(q, int) or q > 4:
                            dve.wait_ge(dst_in, 96)
                        for t in (1, 0):
                            tile = (NPAIR - 1 - q) * 2 + t
                            cols = same_all[:, tile * P:(tile + 1) * P] if isinstance(q, int) else same_all[:, bass.ds(tile * P, P)]
                            of = dflat[:, tile:tile + 1] if isinstance(q, int) else dflat[:, bass.ds(tile, 1)]
                            nc.vector.tensor_scalar(cols, cols, of, None, ALU.is_equal).then_inc(same_ready, 1)
                    if within(q, 2, NPAIR + 2):
                        dve.wait_ge(summed[0], edge_count(l, q - 2))
                        wait(dve, tot_ready[0], edge_count(l, q - 3))
                        nc.vector.tensor_copy(aggT[:, 0, :], bank[5][0:MR, :]).then_inc(summed_out[0], 1)
                    if not within(q, 0, NPAIR):
                        return
                    dve.wait_ge(meta_in[k], slot_count(l, k, turn) * 16)
                    sh = meta[:, k, 6:14].rearrange("p (t c) -> p t c", t=2)
                    if G == 1:
                        dve.wait_ge(gathered[k], slot_count(l, k, turn) * 32)
                        wait(dve, msg_ready, edge_count(l, q - 1))
                        nc.vector.tensor_tensor(yv[:, k2], sh, xg[:, k, :, F:F + 1].to_broadcast([P, 2, 4]), ALU.mult)\
                            .then_inc(y_ready, 1)
                        y = yv[:, k2]
                        dve.wait_ge(y_ready, edge_count(l, q))
                    else:
                        y = sh
                        wait(dve, msg_ready, edge_count(l, q - 1))
                    dve.wait_ge(w_ready, edge_count(l, q))
                    wt = bank[2][:, 0:384].rearrange("p (t c) -> p t c", t=2)
                    nc.vector.tensor_tensor(wy[:, k2, :, 0, :], wt[:, :, 0:96], y[:, :, 0:1].to_broadcast([P, 2, 96]), ALU.mult)
                    nc.vector.tensor_tensor(wy[:, k2, :, 1:4, :],
                                            wt[:, :, None, 96:192].to_broadcast([P, 2, 3, 96]),
                                            y[:, :, 1:4, None].to_broadcast([P, 2, 3, 96]), ALU.mult).then_inc(wy_ready, 1)
                    if G == 1:
                        dve.wait_ge(f_ready, edge_count(l, q))
                        f = bank[3][:, 0:2 * F].rearrange("p (t c) -> p t c", t=2)
                    else:
                        dve.wait_ge(fa_out, q + 1)
                        for t in range(2):
                            last = nc.vector.scalar_tensor_tensor(out=fsum[:, k2, t, :], in0=bank[3 + t][:, F:2 * F],
                                                                  scalar=xg[:, k, t, F + 1:F + 2], in1=fsum[:, k2, t, :],
                                                                  op0=ALU.mult, op1=ALU.add)
                        last.then_inc(f_summed, 1)
                        dve.wait_ge(f_summed, q + 1)
                        f = fsum[:, k2]
                    dve.wait_ge(wy_ready, edge_count(l, q))
                    fv = f[:, :, S:F].rearrange("p t (d v) -> p t d v", d=3)
                    nc.vector.tensor_tensor(dprod[:, :, :, :], wy[:, k2, :, 1:4, S:96], fv, ALU.mult).then_inc(dprod_ready, 1)
                    nc.vector.tensor_tensor(msg[:, k2, :, :, 1:1 + S], wy[:, k2, :, :, 0:S],
                                            f[:, :, None, 0:S].to_broadcast([P, 2, 4, S]), ALU.mult)
                    nc.vector.tensor_tensor(msg[:, k2, :, 1:4, 1 + S:97],
                                            wy[:, k2, :, 0:1, S:96].to_broadcast([P, 2, 3, V]), fv, ALU.mult)
                    nc.vector.tensor_copy(msg[:, k2, :, :, 0], meta[:, k, 4:6, None].to_broadcast([P, 2, 4]))
                    dve.wait_ge(dprod_ready, edge_count(l, q))
                    nc.vector.tensor_reduce(msg[:, k2, :, 0, 1 + S:97], dprod[:, :, :, :].rearrange("p t d v -> p t v d"),
                                            AX.X, ALU.add).then_inc(msg_ready, 1)

                steps(dve, 0, NPAIR + 2, EDGE_STEADY, edge_vectors)

                def node_bank(k, d, t):
                    return (bank[2 + (2 * k + d) % 6], t * F) if G == 1 else (bank[2 + (4 * k + 2 * d + t) % 6], 0)

                def node_vectors(b, k, turn):
                    k2 = k % 2
                    base = b * 2 + 2 * l * NBLK
                    kk, tt = back(k, turn, 1, NRING)
                    v, (y, a, c) = var[:, kk % 2], (newton[:, kk % 2, n] for n in range(3))
                    R = rstd[:, kk, :]
                    stt = nc.vector.scalar_tensor_tensor
                    ops = [lambda: nc.vector.tensor_scalar(v, mv[:, kk, :, 1], EPS, None, ALU.add),
                           lambda: nc.vector.tensor_scalar(y.bitcast(i32), v.bitcast(i32), -0.5, GUESS, ALU.mult, ALU.add)]
                    for n in range(3):
                        ops += [lambda: stt(out=a, in0=y, scalar=-0.5, in1=v, op0=ALU.mult, op1=ALU.mult),
                                lambda: nc.vector.tensor_tensor(c, a, y, ALU.mult),
                                lambda to=y if n < 2 else R: stt(out=to, in0=c, scalar=1.5, in1=y, op0=ALU.add, op1=ALU.mult)]
                    ops.append(lambda: stt(out=shift[:, kk, :], in0=mv[:, kk, :, 0], scalar=-1.0, in1=R,
                                           op0=ALU.mult, op1=ALU.mult))
                    done = [0]
                    rooted = l == 0 and within(b, 1, NBLK + 1)

                    def root(n=1):
                        for _ in range(n):
                            i = done[0]
                            if not rooted or i > ROOT_OPS:
                                return
                            if i == 0:
                                dve.wait_ge(mv_ready, b)
                                wait(dve, normed, b - NRING)
                            else:
                                dve.wait_ge(root_chain, (b - 1) * ROOT_OPS + i)
                            ops[i]().then_inc(root_chain if i < ROOT_OPS else shift_ready, 1)
                            done[0] += 1

                    def inverse_count(b, k, turn):
                        dve.wait_ge(a_in[k], node_slot(l, k, turn) * 16)
                        nc.vector.tensor_scalar(inv_count[:, k, 0, :], an[:, k, :, 1], 1.0, None, ALU.max).then_inc(count_max, 1)
                        root()
                        dve.wait_ge(count_max, b + 1)
                        nc.vector.reciprocal(inv_count[:, k, 1, :], inv_count[:, k, 0, :]).then_inc(count_ready, 1)

                    k3, t3 = back(k, turn, 3, NRING)

                    def inverse_three_before():
                        if l and within(b, 3, NBLK + 3):
                            dve.wait_ge(std_ready, b + ((l - 1) * NBLK - 2))
                            nc.vector.reciprocal(rstd[:, k3, :], std[:, k3, :]).then_inc(inverse_ready, 1)

                    def shift_three_before():
                        if l and within(b, 3, NBLK + 3):
                            dve.wait_ge(inverse_ready, b + ((l - 1) * NBLK - 2))
                            stt(out=shift[:, k3, :], in0=mv[:, k3, :, 0], scalar=-1.0, in1=rstd[:, k3, :],
                                op0=ALU.mult, op1=ALU.mult).then_inc(shift_ready, 1)

                    inverse_three_before()
                    if not within(b, 0, NBLK):
                        shift_three_before()
                    if within(b, 0, NBLK):
                        if l == 2 and isinstance(b, int) and b == 0:
                            inverse_count(b, k, turn)
                        if l == 2 and within(b, 0, NBLK - 1):
                            inverse_count(b + 1, (k + 1) % NRING, turn + (k + 1) // NRING)
                        dve.wait_ge(x_in[k], node_slot(l, k, turn) * 16)
                        if l == 0:
                            dve.wait_ge(gates_ready, b + 1)
                        wait(dve, stored[k], node_slot(l, k, turn - 1) * 16)
                        alone(dve, passed["dve"])
                        for d in range(2):
                            for g in range(G):
                                if g == 0:
                                    dve.wait_ge(sc_ready, base + (d + 1))
                                else:
                                    dve.wait_ge(y_part, b * 2 + (d + 1))
                                for t in range(2):
                                    j = 2 * d + t
                                    gate = gates[:, k, j, 1:2] if l == 0 else xn[:, k, j, F + g:F + g + 1]
                                    ob, o = node_bank(k, d, t)
                                    last = stt(out=yn[:, k, j, 0:F], in0=ob[:, o + g * F:o + (g + 1) * F], scalar=gate,
                                               in1=(xn if g == 0 else yn)[:, k, j, 0:F], op0=ALU.mult, op1=ALU.add)
                                    if t == 1:
                                        last.then_inc(y_stt if g == G - 1 else y_part, 1)
                                    root()
                                    if j == 0 and g == 0:
                                        shift_three_before()
                        if l == 1:
                            dve.wait_ge(y_stt, base + 2)
                            dve.sem_inc(y_sum, 1)
                        else:
                            if G == 1:
                                dve.wait_ge(gated, b + (1 if l == 0 else NBLK + 1))
                            else:
                                dve.wait_ge(pair_summed, b + 1)
                            dve.wait_ge(y_stt, base + 2)
                            gated_sums = an[:, k, :, 2:AW] if G == 1 else an3[:, k, :, 0:F]
                            nc.vector.tensor_tensor(yn[:, k, :, 0:F], yn[:, k, :, 0:F], gated_sums, ALU.add).then_inc(y_sum, 1)
                        root()
                        dve.wait_ge(y_sum, node_count(l, b))
                        for j in range(BT):
                            last = nc.vector.bn_stats(stats[:, k2, j, :], yn[:, k, j, 0:F])
                            if j == BT - 1:
                                last.then_inc(stats_ready, 1)
                            root()
                    if within(b, 0, NBLK):
                        dve.wait_ge(stats_ready, node_count(l, b))
                        alone(dve, passed["dve"])
                        for j in range(BT):
                            last = nc.vector.bn_aggr(mv[:, k, j, :], stats[:, k2, j, :])
                            if j == BT - 1:
                                last.then_inc(mv_ready, 1)
                            root()
                    root(ROOT_OPS + 1)

                steps(dve, 0, NBLK + (3 if l else 1), NODE_STEADY, node_vectors, NRING)





def kernel(**inputs):
    import concourse.bacc as bacc
    from concourse.bass_utils import run_bass_kernel_spmd

    a = {n: np.asarray(v) for n, v in inputs.items()}
    rows = lambda n, fill=0: np.full((n, 1), fill)
    nodes = np.concatenate([a["x"], a["node_vec1"], a["node_vec1_n2"], a["node_vec1_n3"],
                            np.zeros((N_NODES, 1), np.float32)], axis=1)
    nodes = np.concatenate([nodes, np.zeros((NP - N_NODES, XW), np.float32)], axis=0)
    pad = EP - N_EDGES
    pairs = np.stack([np.concatenate([a["src"], np.zeros(pad, np.int32)]),
                      np.concatenate([a["dst"], np.full(pad, N_NODES, np.int32)])], axis=1)
    eattr = np.concatenate([a["edge_attr_4"], a["edge_attr_8"], a["edge_attr_10"], a["edge_attr_16"]], axis=1)
    eattr = np.concatenate([eattr, np.zeros((pad, EA), np.float32)], axis=0)
    arrays = {"nodes": nodes, "pairs": pairs, "eattr": eattr, **{n: a[n] for n in WEIGHTS}}
    arrays = {n: np.ascontiguousarray(v) for n, v in arrays.items()}

    nc = bacc.Bacc("TRN2", target_bir_lowering=False, num_devices=1)
    given = {n: nc.dram_tensor(n, v.shape, mybir.dt.from_np(v.dtype), kind="ExternalInput").ap()
             for n, v in arrays.items()}
    out = nc.dram_tensor("out", (NP, F), mybir.dt.float32, kind="ExternalOutput").ap()
    build(nc, given["nodes"], given["pairs"], given["eattr"], given, out)
    got = run_bass_kernel_spmd(nc, [arrays], core_ids=[0])
    return got.results[0]["out"][:N_NODES]
```
